# Optimizing a Trainium2 kernel written in Bass

```python
import numpy as np
import jax
import jax.numpy as jnp

def _softmax(x, axis=-1):
    return jax.nn.softmax(x, axis=axis)

def _gelu(x):
    return jax.nn.gelu(x, approximate=True)

def _silu(x):
    return jax.nn.silu(x)

def _sigmoid(x):
    return jax.nn.sigmoid(x)

def _layernorm(x, axis=-1, eps=1e-05):
    m = jnp.mean(x, axis=axis, keepdims=True)
    v = jnp.var(x, axis=axis, keepdims=True)
    return (x - m) / jnp.sqrt(v + eps)

def _scatter_add(tgt, idx, src, axis=0):
    return tgt.at[idx].add(src)

def _segment_sum(src, seg, n):
    return jax.ops.segment_sum(src, seg, n)
kernel_name = 'mk_conv_seq_d2_conv_nhwc256_r4_bc2a24'

def setup_inputs(seed: int=0):
    np.random.seed(seed)
    _w = jnp.asarray

    def _rec_inputs():
        import jax
        import jax.numpy as jnp
        _gk = jax.random.key(seed)
        x = -0.0002091 + 1 * jax.random.normal(jax.random.fold_in(_gk, 1), (32, 56, 56, 64), jnp.float32)
        return x
    x = _rec_inputs()

    def _L0_conv_setup():
        import jax, jax.numpy as jnp
        import numpy as np
        from jax import lax
        BITW = 1
        BITA = 3

        def _ste_round(x, n):
            return x + lax.stop_gradient(jnp.round(x * n) / n - x)

        def _quantize_active(x, bitA):
            x = jnp.minimum(1.0, jnp.abs(x))
            if bitA == 32:
                return x
            n = float(2 ** bitA - 1)
            return _ste_round(x, n)

        def _quantize_weight(w, bitW):
            if bitW == 32:
                return w
            if bitW == 1:
                E = lax.stop_gradient(jnp.mean(jnp.abs(w)))
                y = w / E
                return (y + lax.stop_gradient(jnp.sign(y) - y)) * E
            n = float(2 ** bitW - 1)
            w = jnp.clip(w * 0.5 + 0.5, 0.0, 1.0)
            return 2.0 * _ste_round(w, n) - 1.0
        key = jax.random.key(seed)
        kx, kw, kb = jax.random.split(key, 3)
        x = jax.random.normal(kx, (32, 56, 56, 64), dtype=jnp.float32)
        W = jax.random.normal(kw, (3, 3, 64, 64), dtype=jnp.float32) * 0.02
        b = jax.random.normal(kb, (64,), dtype=jnp.float32) * 0.01
        return {'x': x, 'W': W, 'b': b}
    _L0_conv_all = _L0_conv_setup()
    _L0_conv_in = {k: v for k, v in _L0_conv_all.items() if k in ('W', 'b')}
    del _L0_conv_all

    def _L1_conv_setup():
        import jax, jax.numpy as jnp
        import numpy as np
        N_WIN = 7
        NUM_HEADS = 8
        TOPK = 4
        EPS = 1e-05

        def layernorm(x, g, b):
            mu = x.mean(-1, keepdims=True)
            var = ((x - mu) ** 2).mean(-1, keepdims=True)
            return (x - mu) * jax.lax.rsqrt(var + EPS) * g + b

        def bilevel_routing_attn(x, wqkv, bqkv, wo, bo):
            B, H, W, C = x.shape
            h, w = (H // N_WIN, W // N_WIN)
            R, r = (N_WIN * N_WIN, h * w)
            d = C // NUM_HEADS
            scale = 1.0 / jnp.sqrt(jnp.asarray(d, x.dtype))
            qkv = x @ wqkv + bqkv
            q, k, v = jnp.split(qkv, 3, axis=-1)

            def to_regions(t):
                t = t.reshape(B, N_WIN, h, N_WIN, w, C).transpose(0, 1, 3, 2, 4, 5)
                return t.reshape(B, R, r, C)
            qr, kr, vr = (to_regions(q), to_regions(k), to_regions(v))
            q_reg = qr.mean(2)
            k_reg = kr.mean(2)
            logits = jnp.einsum('brc,bsc->brs', q_reg, k_reg)
            _, idx = jax.lax.top_k(logits, TOPK)
            idx_e = idx[:, :, :, None, None]
            kg = jnp.take_along_axis(kr[:, None], idx_e, axis=2).reshape(B, R, TOPK * r, C)
            vg = jnp.take_along_axis(vr[:, None], idx_e, axis=2).reshape(B, R, TOPK * r, C)
            qh = qr.reshape(B, R, r, NUM_HEADS, d)
            kh = kg.reshape(B, R, TOPK * r, NUM_HEADS, d)
            vh = vg.reshape(B, R, TOPK * r, NUM_HEADS, d)
            scores = jnp.einsum('brqhd,brkhd->brhqk', qh, kh) * scale
            attn = jax.nn.softmax(scores, axis=-1)
            out = jnp.einsum('brhqk,brkhd->brqhd', attn, vh).reshape(B, R, r, C)
            out = out.reshape(B, N_WIN, N_WIN, h, w, C).transpose(0, 1, 3, 2, 4, 5)
            out = out.reshape(B, H, W, C)
            return out @ wo + bo

        def mlp(x, w1, bm1, w2, bm2):
            return jax.nn.gelu(x @ w1 + bm1) @ w2 + bm2
        key = jax.random.key(seed)
        ks = jax.random.split(key, 5)
        C = 64
        s = lambda fan: 1.0 / np.sqrt(fan)
        return {'x': jax.random.normal(ks[0], (8, 56, 56, C), jnp.float32), 'ln1_g': jnp.ones((C,), jnp.float32), 'ln1_b': jnp.zeros((C,), jnp.float32), 'wqkv': jax.random.normal(ks[1], (C, 3 * C), jnp.float32) * s(C), 'bqkv': jnp.zeros((3 * C,), jnp.float32), 'wo': jax.random.normal(ks[2], (C, C), jnp.float32) * s(C), 'bo': jnp.zeros((C,), jnp.float32), 'ln2_g': jnp.ones((C,), jnp.float32), 'ln2_b': jnp.zeros((C,), jnp.float32), 'w1': jax.random.normal(ks[3], (C, 4 * C), jnp.float32) * s(C), 'bm1': jnp.zeros((4 * C,), jnp.float32), 'w2': jax.random.normal(ks[4], (4 * C, C), jnp.float32) * s(4 * C), 'bm2': jnp.zeros((C,), jnp.float32)}
    _L1_conv_all = _L1_conv_setup()
    _L1_conv_in = {k: v for k, v in _L1_conv_all.items() if k in ('ln1_g', 'ln1_b', 'wqkv', 'bqkv', 'wo', 'bo', 'ln2_g', 'ln2_b', 'w1', 'bm1', 'w2', 'bm2')}
    del _L1_conv_all
    return {'x': x, 'L0_conv_W': _L0_conv_in['W'], 'L0_conv_b': _L0_conv_in['b'], 'L1_conv_ln1_g': _L1_conv_in['ln1_g'], 'L1_conv_ln1_b': _L1_conv_in['ln1_b'], 'L1_conv_wqkv': _L1_conv_in['wqkv'], 'L1_conv_bqkv': _L1_conv_in['bqkv'], 'L1_conv_wo': _L1_conv_in['wo'], 'L1_conv_bo': _L1_conv_in['bo'], 'L1_conv_ln2_g': _L1_conv_in['ln2_g'], 'L1_conv_ln2_b': _L1_conv_in['ln2_b'], 'L1_conv_w1': _L1_conv_in['w1'], 'L1_conv_bm1': _L1_conv_in['bm1'], 'L1_conv_w2': _L1_conv_in['w2'], 'L1_conv_bm2': _L1_conv_in['bm2']}

def reference(x, L0_conv_W, L0_conv_b, L1_conv_ln1_g, L1_conv_ln1_b, L1_conv_wqkv, L1_conv_bqkv, L1_conv_wo, L1_conv_bo, L1_conv_ln2_g, L1_conv_ln2_b, L1_conv_w1, L1_conv_bm1, L1_conv_w2, L1_conv_bm2):
    import jax
    import jax.numpy as jnp

    def _L0_conv_ref(x, W, b):
        import jax, jax.numpy as jnp
        import numpy as np
        from jax import lax
        BITW = 1
        BITA = 3

        def _ste_round(x, n):
            return x + lax.stop_gradient(jnp.round(x * n) / n - x)

        def _quantize_active(x, bitA):
            x = jnp.minimum(1.0, jnp.abs(x))
            if bitA == 32:
                return x
            n = float(2 ** bitA - 1)
            return _ste_round(x, n)

        def _quantize_weight(w, bitW):
            if bitW == 32:
                return w
            if bitW == 1:
                E = lax.stop_gradient(jnp.mean(jnp.abs(w)))
                y = w / E
                return (y + lax.stop_gradient(jnp.sign(y) - y)) * E
            n = float(2 ** bitW - 1)
            w = jnp.clip(w * 0.5 + 0.5, 0.0, 1.0)
            return 2.0 * _ste_round(w, n) - 1.0
        xq = _quantize_active(x, BITA)
        wq = _quantize_weight(W, BITW)
        out = lax.conv_general_dilated(xq, wq, window_strides=(1, 1), padding='SAME', dimension_numbers=('NHWC', 'HWIO', 'NHWC'))
        return out + b

    def _L1_conv_ref(x, ln1_g, ln1_b, wqkv, bqkv, wo, bo, ln2_g, ln2_b, w1, bm1, w2, bm2):
        import jax, jax.numpy as jnp
        import numpy as np
        N_WIN = 7
        NUM_HEADS = 8
        TOPK = 4
        EPS = 1e-05

        def layernorm(x, g, b):
            mu = x.mean(-1, keepdims=True)
            var = ((x - mu) ** 2).mean(-1, keepdims=True)
            return (x - mu) * jax.lax.rsqrt(var + EPS) * g + b

        def bilevel_routing_attn(x, wqkv, bqkv, wo, bo):
            B, H, W, C = x.shape
            h, w = (H // N_WIN, W // N_WIN)
            R, r = (N_WIN * N_WIN, h * w)
            d = C // NUM_HEADS
            scale = 1.0 / jnp.sqrt(jnp.asarray(d, x.dtype))
            qkv = x @ wqkv + bqkv
            q, k, v = jnp.split(qkv, 3, axis=-1)

            def to_regions(t):
                t = t.reshape(B, N_WIN, h, N_WIN, w, C).transpose(0, 1, 3, 2, 4, 5)
                return t.reshape(B, R, r, C)
            qr, kr, vr = (to_regions(q), to_regions(k), to_regions(v))
            q_reg = qr.mean(2)
            k_reg = kr.mean(2)
            logits = jnp.einsum('brc,bsc->brs', q_reg, k_reg)
            _, idx = jax.lax.top_k(logits, TOPK)
            idx_e = idx[:, :, :, None, None]
            kg = jnp.take_along_axis(kr[:, None], idx_e, axis=2).reshape(B, R, TOPK * r, C)
            vg = jnp.take_along_axis(vr[:, None], idx_e, axis=2).reshape(B, R, TOPK * r, C)
            qh = qr.reshape(B, R, r, NUM_HEADS, d)
            kh = kg.reshape(B, R, TOPK * r, NUM_HEADS, d)
            vh = vg.reshape(B, R, TOPK * r, NUM_HEADS, d)
            scores = jnp.einsum('brqhd,brkhd->brhqk', qh, kh) * scale
            attn = jax.nn.softmax(scores, axis=-1)
            out = jnp.einsum('brhqk,brkhd->brqhd', attn, vh).reshape(B, R, r, C)
            out = out.reshape(B, N_WIN, N_WIN, h, w, C).transpose(0, 1, 3, 2, 4, 5)
            out = out.reshape(B, H, W, C)
            return out @ wo + bo

        def mlp(x, w1, bm1, w2, bm2):
            return jax.nn.gelu(x @ w1 + bm1) @ w2 + bm2
        x = x + bilevel_routing_attn(layernorm(x, ln1_g, ln1_b), wqkv, bqkv, wo, bo)
        x = x + mlp(layernorm(x, ln2_g, ln2_b), w1, bm1, w2, bm2)
        return x

    def _gn(v, G=32, eps=1e-05):
        B_, H_, W_, C_ = v.shape
        g = v.reshape(B_, H_, W_, G, C_ // G)
        m = jnp.mean(g, axis=(1, 2, 4), keepdims=True)
        s = jnp.var(g, axis=(1, 2, 4), keepdims=True)
        return ((g - m) / jnp.sqrt(s + eps)).reshape(v.shape)

    def _ln_c(v, eps=1e-06):
        m = jnp.mean(v, axis=-1, keepdims=True)
        s = jnp.var(v, axis=-1, keepdims=True)
        return (v - m) / jnp.sqrt(s + eps)

    def _ln_t(v, eps=1e-05):
        m = jnp.mean(v, axis=-1, keepdims=True)
        s = jnp.var(v, axis=-1, keepdims=True)
        return (v - m) / jnp.sqrt(s + eps)

    def _to_tokens(v):
        B_, H_, W_, C_ = v.shape
        return v.reshape(B_, H_ * W_, C_)

    def _from_tokens(t, like):
        return t.reshape(like.shape)
    x = _L0_conv_ref(x, L0_conv_W, L0_conv_b)
    x = _L1_conv_ref(x, L1_conv_ln1_g, L1_conv_ln1_b, L1_conv_wqkv, L1_conv_bqkv, L1_conv_wo, L1_conv_bo, L1_conv_ln2_g, L1_conv_ln2_b, L1_conv_w1, L1_conv_bm1, L1_conv_w2, L1_conv_bm2)
    return x

_drawn_inputs = setup_inputs


def setup_inputs(seed=0):
    import zlib

    import numpy as np

    out = dict(_drawn_inputs(seed))
    spreads = {'L1_conv_ln1_g': (1.0, 0.2),
     'L1_conv_ln1_b': (0.0, 0.1),
     'L1_conv_bqkv': (0.0, 0.1),
     'L1_conv_bo': (0.0, 0.1),
     'L1_conv_ln2_g': (1.0, 0.2),
     'L1_conv_ln2_b': (0.0, 0.1),
     'L1_conv_bm1': (0.0, 0.1),
     'L1_conv_bm2': (0.0, 0.1)}
    factors = {}
    for name, (base, spread) in spreads.items():
        noise = np.random.default_rng([zlib.crc32(name.encode()), seed]).standard_normal(out[name].shape)
        drawn = base * np.exp(spread * noise) if base else spread * noise
        out[name] = jnp.asarray(drawn.astype(out[name].dtype))
    for name, factor in factors.items():
        out[name] = (out[name] * factor).astype(out[name].dtype)
    return out
```

```python
from contextlib import ExitStack

import concourse.bass as bass
from concourse import mybir
from concourse.alu_op_type import AluOpType as ALU

ACT = mybir.ActivationFunctionType
AX = mybir.AxisListType
F32 = mybir.dt.float32
F32R = mybir.dt.float32r
BF16 = mybir.dt.bfloat16
U32 = mybir.dt.uint32

C = 64
IMG = 56
NW = 7
WS = IMG // NW
R = NW * NW
RT = WS * WS
ST = NW * RT
HEADS = 8
HD = C // HEADS
TOPK = 4
KEYS = TOPK * RT
PADW = IMG + 2
XP = 2 * IMG
XK = IMG // 2
RND = 12582912.0
LEVELS = 7.0
EPS = 1e-5
HG = 4
NG = HEADS // HG
QR = HG * HD
NP3 = 3 * QR
VC = 17
RING = 4
STEPS = 2 * NW
OT = ST // 4
HALF = 4


def build(nc, io):
    x, out = io["x"], io["out"]
    PAIRS = x.shape[0] // 2
    with ExitStack() as ctx:
        def sb(name, shape, dt=F32):
            return ctx.enter_context(nc.sbuf_tensor(name, shape, dt))

        def sem(name):
            return ctx.enter_context(nc.semaphore(name))

        ident = sb("ident", [128, 128])
        identb = sb("identb", [128, 128], BF16)
        pick = sb("pick", [128, 128])
        headmask3 = sb("headmask3", [128, 3, HG])
        headmask = sb("headmask", [128, HG])
        mean_w = sb("mean_w", [128, 128])
        wq = sb("wq", [128, 128])
        wk = sb("wk", [128, 128])
        wv = sb("wv", [128, 128])
        w1 = sb("w1", [128, 2, 4 * C])
        w2 = sb("w2", [128, 2, C])
        wo = sb("wo", [128, 2, C])
        wconv = sb("wconv", [128, 9, 128], BF16)
        wsum = sb("wsum", [128, 1])
        cscale = sb("cscale", [128, 1])
        cols = sb("cols", [128, 12])
        bvb = sb("bvb", [128, 2 * C])
        bm2b = sb("bm2b", [128, C])
        epst = sb("epst", [128, 1])
        zero = sb("zero", [128, 1])
        bconv, g1, b1, g2, b2, bq, bk, bo, bm1a, bm1b = (cols[:, i:i + 1] for i in range(10))

        xin_ = sb("xin", [128, 2 * XK * C])
        xin = xin_[0:XP].rearrange("p (h k c) -> p h k c", h=2, c=C)
        xq_ = sb("xq", [128, 4 * ST])
        xq = xq_[0:XP, 0:XK * C].bitcast(BF16).rearrange("p (k n) -> p k n", k=XK)
        xT = sb("xT", [128, PADW, PADW], BF16)
        x1 = sb("x1", [128, NW, ST])
        xn = sb("xn", [128, NW, ST])
        sq = sb("sq", [128, 2, ST])
        wconv_f = sq[:].rearrange("p m b -> p (m b)")[:, 0:9 * C].rearrange("p (m b) -> p m b", b=C)
        lnv = sb("lnv", [128, ST])
        rs = sb("rs", [128, 2, ST])
        qH = sb("qH", [128, NW, ST], F32R)
        qL = sb("qL", [128, NW, ST], F32R)
        k_ = sb("k_", [128, 4, ST])
        kH, kL = k_[:, 0:2].bitcast(F32R), k_[:, 2:4].bitcast(F32R)
        regsum = sb("regsum", [128, 2, R])
        ks = [sb(f"ks{i}", [NP3, R, NG * RT], F32R) for i in range(2)]
        vs = sb("vs", [128, R, 2, 4 * VC])
        lg = sb("lg", [R, 2, R])
        top = sb("top", [R, 2, 8])
        topi = sb("topi", [R, 2, 8], U32)
        idx = sb("idx", [1, 2 * R * TOPK], U32)
        idx_dram = nc.dram_tensor("idx_scratch", [2, R, TOPK], U32, kind="Internal").ap()

        qs = [sb(f"qs{i}", [128, NG, ST], F32R) for i in range(2)]
        kg = [sb(f"kg{i}", [128, NG, TOPK, RT], F32R) for i in range(RING)]
        vg = [sb(f"vg{i}", [128, 2 * 4 * VC + 16]) for i in range(RING)]
        qb = [sb(f"qb{i}", [128, NG, HG, RT], F32R) for i in range(RING)]
        mx = [sb(f"mx{i}", [128, 4], BF16) for i in range(2)]
        pt = [xin_[:, 1024 * i:1024 * i + 1024].rearrange("p (c n) -> p c n", c=2) for i in range(2)]
        wpos, wneg = (xin_[:, 1024 * i:1024 * i + 9 * C].rearrange("p (m b) -> p m b", b=C) for i in range(2))
        x3 = xin_[:, 2048:2048 + ST]
        ot = xin_[0:OT, 2560:3072].rearrange("p (h t c) -> p h t c", h=2, c=C)
        hid = xq_[:].rearrange("p (m t) -> p m t", m=4)
        us = k_[:].rearrange("p (h e) t -> p h e t", h=2)
        ln_s, rc_s = sq, rs
        x2, xc2, sq2, ln2, rs2, xh2, xn2 = (xn[:, i] for i in range(7))

        ps = ctx.enter_context(nc.psum_tensor("ps", [128, 8, 512], F32))

        names = """w_loaded zeroed const_ready diag_ready wabs wsum_full wscale sign_ready zero2
            x_loaded x_abs x_rounded x_ready xt_full xt_ready
            conv_full x1_ready mean_full xc_ready sq_ready var_full lnv_ready rs_ready xh_ready xn_ready
            q_full qH_ready qL_ready k_full kH_ready kL_ready v_full v_ready
            logit_full logit_ready top_ready topi_ready idx_stored idx_loaded qs_ready
            qb_ready vg_ready sm_full mx_ready mt_full mt_ready st_full pt_ready u_full u_ready
            sum_full lns_ready rcs_ready un_ready y_full x2_ready mean2_full xc2_ready sq2_ready
            var2_full lnv2_ready rs2_ready xh2_ready xn2_ready h_full hid_ready o_full x3_ready
            t_full ot_ready out_stored waited qs_late_ready""".split()
        S = {n: sem(n) for n in names}
        ks_stored = [sem("ks_stored0"), sem("ks_stored1")]

        tables = []
        block = ctx.enter_context(nc.Block())

        def chosen(eng, regs, s, i):
            at = (s * NW + i // 2) * TOPK + (i % 2) * R * TOPK
            eng.load(regs, idx[0:1, bass.ds(at, TOPK)])
            return [eng.snap(r, min_val=0, max_val=R - 1) for r in regs]

        def settled(eng):
            eng.sem_inc(S["waited"], 1)

        def load_table(act):
            act.add_instruction(mybir.InstLoadActFuncSet(name=f"I-{4000000 + len(tables)}", act_func_set_id=6, engine=mybir.EngineType.Activation, ins=[], outs=[]))
            tables.append(1)

        @block.sync
        def _(sp):
            for name in 'out_stored'.split():
                sp.sem_inc(S[name], 1)
            for t in ks_stored:
                sp.sem_inc(t, 1)
            n = [0]
            def query_stack(s, part):
                first, last = (0, HALF) if part == "qs_ready" else (HALF, NW)
                cut = slice(first * RT, last * RT)
                for h in range(2):
                    for g in range(NG):
                        rows = slice(64 * h + QR * g, 64 * h + QR * g + QR)
                        for q, src in enumerate((qH, qH, qL)):
                            sp.dma_start(qs[h][QR * q:QR * q + QR, g, cut].bitcast(F32),
                                         src[rows, bass.ds(s, 1), cut].bitcast(F32).rearrange("p o t -> p (o t)")).then_inc(S[part], 16)

            def strip(p, s, last):
                T = p * NW + s
                sp.wait_ge(S["qb_ready"], 1 + T * STEPS)
                query_stack(s, "qs_late_ready")
                if not last:
                    sp.wait_ge(S["qb_ready"], 1 + T * STEPS + 2 * HALF)
                    query_stack(s + 1, "qs_ready")
                sp.wait_ge(S["ot_ready"], 1 + T + 1)
                for h in range(2):
                    dst = out[bass.ds(p * 2 + h, 1), bass.ds(s * WS, WS)].rearrange("o y c k -> (o y c k)")
                    sp.dma_start(dst.rearrange("(p n) -> p n", p=OT), ot[:, h].rearrange("p t c -> p (t c)")).then_inc(S["out_stored"], 16)

            def load(dst, src):
                sp.dma_start(dst, src).then_inc(S["w_loaded"], 16)
                n[0] += 1

            def col(i, src):
                for h in range(2):
                    load(cols[64 * h:64 * h + 64, i:i + 1], src.rearrange("(p o) -> p o", o=1))

            sp.wait_ge(S["zeroed"], 1)
            W = io["L0_conv_W"].rearrange("m b i o -> i (m b) o")
            for h in range(2):
                load(wconv_f[64 * h:64 * h + 64], W)
                d = slice(64 * h, 64 * h + 64)
                load(wq[d, d], io["L1_conv_wqkv"][:, 0:C])
                load(wk[d, d], io["L1_conv_wqkv"][:, C:2 * C])
                load(wv[d, d], io["L1_conv_wqkv"][:, 2 * C:3 * C])
                load(w1[d, h, :], io["L1_conv_w1"])
                load(bvb[:, d], io["L1_conv_bqkv"][2 * C:3 * C].rearrange("(o n) -> o n", o=1).broadcast_to([128, C]))
            col(0, io["L0_conv_b"])
            col(1, io["L1_conv_ln1_g"])
            col(2, io["L1_conv_ln1_b"])
            col(3, io["L1_conv_ln2_g"])
            col(4, io["L1_conv_ln2_b"])
            col(5, io["L1_conv_bqkv"][0:C])
            col(6, io["L1_conv_bqkv"][C:2 * C])
            col(7, io["L1_conv_bo"])
            load(bm2b[:], io["L1_conv_bm2"].rearrange("(o n) -> o n", o=1).broadcast_to([128, C]))
            for m in range(2):
                load(cols[:, 8 + m:9 + m], io["L1_conv_bm1"][128 * m:128 * m + 128].rearrange("(p o) -> p o", o=1))
                load(w2[:, m, :], io["L1_conv_w2"][128 * m:128 * m + 128, :])
            for j in range(4):
                for e in range(2):
                    load(wo[32 * j + 8 * e:32 * j + 8 * e + 8, e, :], io["L1_conv_wo"][16 * j + 8 * e:16 * j + 8 * e + 8, :])
            assert n[0] == WEIGHT_DMAS

            sp.wait_ge(S["sign_ready"], 1)
            with sp.Fori(0, PAIRS) as p:
                sp.wait_ge(S["x_ready"], 1 + p * 2)
                for h in range(2):
                    sp.dma_start(xin[:, h], x[bass.ds(p * 2 + h, 1)].rearrange("o (p y) (h c) k -> (o p y h) c k", y=1, h=2)).then_inc(S["x_loaded"], 16)
                for s in range(NW):
                    sp.wait_ge(S["kL_ready"], 1 + p * NW + s + 1)
                    for h in range(2):
                        for g in range(NG):
                            rows = slice(64 * h + QR * g, 64 * h + QR * g + QR)
                            for q, src in enumerate((kH, kL, kH)):
                                sp.dma_start(ks[h][QR * q:QR * q + QR, s * NW:s * NW + NW, g * RT:g * RT + RT].bitcast(F32),
                                             src[rows, s % 2, :].bitcast(F32).rearrange("p (n t) -> p n t", n=NW)).then_inc(ks_stored[s % 2], 16)
                sp.wait_ge(S["topi_ready"], p + 1)
                for h in range(2):
                    sp.dma_start(idx_dram[h], topi[:, h, 0:TOPK]).then_inc(S["idx_stored"], 16)
                sp.wait_ge(S["idx_stored"], p * 32 + 32)
                sp.dma_start(idx[:], idx_dram.rearrange("(o h) y k -> o (h y k)", o=1)).then_inc(S["idx_loaded"], 16)
                sp.wait_ge(S["idx_loaded"], p * 16 + 16)
                for b in range(2):
                    sp.wait_ge(ks_stored[b], 1 + (p + 1) * (192 * len(range(b, NW, 2))))
                sp.wait_ge(S["qb_ready"], 1 + p * (NW * STEPS))
                query_stack(0, "qs_ready")
                with sp.Fori(0, NW - 1) as s:
                    strip(p, s, False)
                strip(p, NW - 1, True)
            sp.wait_ge(S["out_stored"], 1 + 32 * PAIRS * NW)

        @block.gpsimd
        def _(pool):
            Z = S["zero2"]
            for i, t in enumerate((ident, pick, headmask3)):
                pool.memset(t[:], 1.0 if t is headmask3 else 0.0).then_inc(Z, 1)
            pool.wait_ge(Z, 3)
            pool.affine_select(out=ident[:], in_=ident[:], compare_op=ALU.not_equal, fill=1.0, base=0,
                               pattern=[[-1, 128]], channel_multiplier=1).then_inc(Z, 1)
            v = pick[:].rearrange("p (m b) -> p m b", m=4)
            pool.affine_select(out=v, in_=v, compare_op=ALU.not_equal, fill=1.0, base=-16,
                               pattern=[[-32, 4], [0, 32]], channel_multiplier=1).then_inc(Z, 1)
            pool.affine_select(out=headmask3[:], in_=headmask3[:], compare_op=ALU.is_ge, fill=0.0, base=0,
                               pattern=[[-QR, 3], [-HD, HG]], channel_multiplier=1).then_inc(Z, 1)
            pool.wait_ge(Z, 6)
            pool.affine_select(out=headmask3[:], in_=headmask3[:], compare_op=ALU.is_ge, fill=0.0, base=HD - 1,
                               pattern=[[QR, 3], [HD, HG]], channel_multiplier=-1).then_inc(S["const_ready"], 1)
            pool_regs = [pool.alloc_register(f"pool_region{k}") for k in range(TOPK)]

            def values(p, s, i):
                T = p * NW + s
                pool.wait_ge(S["u_full"], 1 + T * STEPS + max(i - RING + 1, 0))
                for k, region in enumerate(chosen(pool, pool_regs, s, i)):
                    rows = slice(64 * (k % 2), 64 * (k % 2) + 64)
                    j = pool.tensor_copy(vg[i % RING][rows, (k // 2) * 4 * VC:(k // 2 + 1) * 4 * VC],
                                         vs[rows, bass.ds(region, 1), i % 2, :].rearrange("p o n -> p (o n)"))
                j.then_inc(S["vg_ready"], 1)

            with pool.Fori(0, PAIRS) as p:
                pool.wait_ge(S["v_ready"], 1 + p * NW + NW)
                pool.wait_ge(S["idx_loaded"], p * 16 + 16)
                settled(pool)
                with pool.Fori(0, NW) as s:
                    for i in range(STEPS):
                        values(p, s, i)

        @block.vector
        def _(v):
            for name in 'x_ready xc_ready qL_ready kL_ready v_ready qb_ready mx_ready ot_ready'.split():
                v.sem_inc(S[name], 1)
            ch = [0]
            v_regs = [v.alloc_register(f"v_region{k}") for k in range(TOPK)]

            def link(ins):
                ch[0] += 1
                ins.then_inc(S["diag_ready"], 1)
                v.wait_ge(S["diag_ready"], ch[0])

            for t in (wq, wk, wv, w1, wo, mean_w):
                v.memset(t[:], 0.0)
            v.memset(zero[:], 0.0)
            v.memset(epst[:], EPS)
            v.memset(wconv[:], 0.0)
            v.memset(xT[:], 0.0)
            v.memset(vs[:], 1.0)
            for t in kg:
                v.memset(t[:].bitcast(F32), -1.0)
            for t in vg:
                v.memset(t[:], 1.0)
            for t in qs:
                v.memset(t[NP3:128].bitcast(F32), 0.0)
            link(v.memset(mx[0][:], 0.0))
            v.memset(mean_w[0:64, 0:64], 1.0 / C)
            v.memset(mean_w[64:128, 64:128], 1.0 / C).then_inc(S["zeroed"], 1)
            v.wait_ge(S["const_ready"], 1)
            v.tensor_copy(identb[:], ident[:])
            link(v.tensor_reduce(headmask[:], headmask3[:].rearrange("p m b -> p b m"), AX.X, ALU.add))
            v.wait_ge(S["w_loaded"], 16 * WEIGHT_DMAS)
            v.tensor_reduce(wsum[:], wconv_f[:].rearrange("p m b -> p (m b)"), AX.X, ALU.add, apply_absolute_value=True).then_inc(S["wabs"], 1)
            v.tensor_scalar(wpos[:], wconv_f[:], 0.0, None, ALU.is_gt)
            link(v.tensor_scalar(wneg[:], wconv_f[:], 0.0, None, ALU.is_lt))
            for h in range(2):
                d = slice(64 * h, 64 * h + 64)
                i = v.tensor_tensor(wconv[d, :, d], wpos[d], wneg[d], ALU.subtract)
            i.then_inc(S["sign_ready"], 1)
            v.wait_ge(S["wsum_full"], 1)
            v.tensor_scalar(cscale[:], ps[:, 0, 0:1], 1.0 / (9 * C), 1.0 / LEVELS, ALU.mult, ALU.mult).then_inc(S["wscale"], 1)

            with v.Fori(0, PAIRS) as p:
                for h in range(2):
                    v.wait_ge(S["x_abs"], p * 2 + h + 1)
                    v.tensor_scalar(xin[:, h], xin[:, h], LEVELS, RND, ALU.min, ALU.add).then_inc(S["x_rounded"], 1)
                    v.wait_ge(S["x_rounded"], p * 2 + h + 1)
                    v.tensor_scalar(xq[:, :, C * h:C * h + C], xin[:, h], RND, None, ALU.subtract).then_inc(S["x_ready"], 1)
                for t in range(NW + 3):
                    if 0 <= t - 1 < NW:
                        s = t - 1
                        v.wait_ge(S["mean_full"], p * NW + s + 1)
                        v.tensor_tensor(xn[:, s], x1[:, s], ps[:, 1, 0:ST], ALU.subtract).then_inc(S["xc_ready"], 1)
                    if 0 <= t - 2 < NW:
                        s = t - 2
                        v.wait_ge(S["rs_ready"], 1 + p * NW + s + 1)
                        v.tensor_tensor(xn[:, s], xn[:, s], rs[:, s % 2], ALU.mult).then_inc(S["xh_ready"], 1)
                        v.wait_ge(S["xh_ready"], p * NW + s + 1)
                        v.tensor_scalar(xn[:, s], xn[:, s], g1, b1, ALU.mult, ALU.add).then_inc(S["xn_ready"], 1)
                    if 0 <= t - 3 < NW:
                        s = t - 3
                        n = p * NW + s + 1
                        v.wait_ge(S["qH_ready"], n)
                        v.tensor_reduce(regsum[:, 0, s * NW:s * NW + NW], ps[:, 3, 0:ST].rearrange("p (n t) -> p n t", n=NW), AX.X, ALU.add)
                        v.scalar_tensor_tensor(qL[:, s], ps[:, 3, 0:ST], bq, qH[:, s].bitcast(F32), ALU.add, ALU.subtract).then_inc(S["qL_ready"], 1)
                        v.wait_ge(S["kH_ready"], n)
                        v.tensor_reduce(regsum[:, 1, s * NW:s * NW + NW], ps[:, 4, 0:ST].rearrange("p (n t) -> p n t", n=NW), AX.X, ALU.add)
                        v.scalar_tensor_tensor(kL[:, s % 2], ps[:, 4, 0:ST], bk, kH[:, s % 2].bitcast(F32), ALU.add, ALU.subtract).then_inc(S["kL_ready"], 1)
                        v.wait_ge(S["v_full"], n)
                        for b, r0, nr in ((5, 0, 4), (6, 4, 3)):
                            i = v.tensor_tensor(
                                vs[:, s * NW + r0:s * NW + r0 + nr].rearrange("p y h (j c) -> p y (h j) c", c=VC)[:, :, :, 0:16],
                                ps[:, b, 0:128 * nr].rearrange("p (y j c) -> p y j c", y=nr, c=16),
                                bvb[:].rearrange("p (j c) -> p j c", c=16).unsqueeze(1).broadcast_to([128, nr, 8, 16]), ALU.add)
                        i.then_inc(S["v_ready"], 1)
                v.wait_ge(S["kL_ready"], 1 + p * NW + NW)
                v.scalar_tensor_tensor(regsum[:, 0], bq.broadcast_to([128, R]), float(RT), regsum[:, 0], ALU.mult, ALU.add)
                v.scalar_tensor_tensor(regsum[:, 1], bk.broadcast_to([128, R]), float(RT), regsum[:, 1], ALU.mult, ALU.add).then_inc(S["logit_ready"], 1)
                v.wait_ge(S["logit_full"], p + 1)
                v.tensor_copy(lg[:], ps[0:R, 0:2, 0:R]).then_inc(S["logit_ready"], 1)
                v.wait_ge(S["logit_ready"], p * 2 + 2)
                settled(v)
                for h in range(2):
                    v.max(top[:, h], lg[:, h]).then_inc(S["top_ready"], 1)
                v.wait_ge(S["top_ready"], p * 2 + 2)
                settled(v)
                for h in range(2):
                    i = v.max_index(topi[:, h], top[:, h], lg[:, h])
                i.then_inc(S["topi_ready"], 1)
                v.wait_ge(S["idx_loaded"], p * 16 + 16)
                for b in range(2):
                    v.wait_ge(ks_stored[b], 1 + (p + 1) * (192 * len(range(b, NW, 2))))
                settled(v)

                with v.Fori(0, NW) as s:
                    T = p * NW + s

                    def queries(i):
                        v.wait_ge(S["st_full"], 1 + (T * STEPS + max(i - RING + 1, 0)) * 2)
                        if i == 2 * HALF:
                            v.wait_ge(S["qs_late_ready"], (T + 1) * (16 * 12))
                        q = qs[i % 2][:, :, (i // 2) * RT:(i // 2) * RT + RT].bitcast(F32)
                        for g in range(NG):
                            v.tensor_tensor(qb[i % RING][:, g],
                                            q[:, g].unsqueeze(1).broadcast_to([128, HG, RT]),
                                            headmask[:].unsqueeze(2).broadcast_to([128, HG, RT]), ALU.mult)
                        for k, region in enumerate(chosen(v, v_regs, s, i)):
                            j = v.tensor_copy(kg[i % RING][0:NP3, :, k, :],
                                              ks[i % 2][:, bass.ds(region, 1), :].rearrange("p o (g t) -> p (o g) t", g=NG))
                        j.then_inc(S["qb_ready"], 1)

                    v.wait_ge(S["qs_ready"], (T + 1) * (16 * 12))
                    queries(0)
                    queries(1)
                    for t in range(STEPS):
                        v.wait_ge(S["sm_full"], T * STEPS + t + 1)
                        v.wait_ge(S["mt_full"], 1 + T * STEPS + max(t - 1, 0))
                        v.tensor_reduce(mx[t % 2][:].rearrange("p (g j) -> p g j", g=2),
                                        ps[:, 0:2, :].rearrange("p g (j k) -> p g j k", j=2), AX.X, ALU.max).then_inc(S["mx_ready"], 1)
                        if t + 2 < STEPS:
                            queries(t + 2)

                    for i in range(4):
                        h, e = i // 2, i % 2
                        v.wait_ge(S["rcs_ready"], T * 4 + i + 1)
                        v.tensor_tensor(us[:, h, e], us[:, h, e], rc_s[:, i % 2], ALU.mult).then_inc(S["un_ready"], 1)
                    v.wait_ge(S["y_full"], T + 1)
                    v.scalar_tensor_tensor(x2[:], ps[:, 4, 0:ST], bo, x1[:, bass.ds(s, 1), :].rearrange("p o t -> p (o t)"), ALU.add, ALU.add).then_inc(S["x2_ready"], 1)
                    v.wait_ge(S["mean2_full"], T + 1)
                    v.tensor_tensor(xc2[:], x2[:], ps[:, 5, 0:ST], ALU.subtract).then_inc(S["xc2_ready"], 1)
                    v.wait_ge(S["rs2_ready"], T + 1)
                    v.tensor_tensor(xh2[:], xc2[:], rs2[:], ALU.mult).then_inc(S["xh2_ready"], 1)
                    v.wait_ge(S["xh2_ready"], T + 1)
                    v.tensor_scalar(xn2[:], xh2[:], g2, b2, ALU.mult, ALU.add).then_inc(S["xn2_ready"], 1)
                    v.wait_ge(S["o_full"], T + 1)
                    for h in range(2):
                        def halves(t):
                            return t.rearrange("p (n y h t) -> p n y h t", n=NW, y=WS, h=2)[:, :, :, h, :]
                        i = v.tensor_tensor(x3[:].rearrange("p (t y n h) -> p n y h t", t=4, y=WS, n=NW)[:, :, :, h, :],
                                            halves(ps[:, 4, 0:ST]), halves(x2[:]), ALU.add)
                    i.then_inc(S["x3_ready"], 1)
                    v.wait_ge(S["t_full"], T + 1)
                    v.wait_ge(S["out_stored"], 1 + T * 32)
                    for h in range(2):
                        i = v.tensor_tensor(ot[:, h], ps[0:OT, 5, :].rearrange("p (t h c) -> p h t c", t=4, h=2)[:, h],
                                            bm2b[0:OT].unsqueeze(1).broadcast_to([OT, 4, C]), ALU.add)
                    i.then_inc(S["ot_ready"], 1)

        @block.scalar
        def _(act):
            for name in 'x1_ready lnv_ready rs_ready u_ready pt_ready mt_ready'.split():
                act.sem_inc(S[name], 1)
            load_table(act)
            act.wait_ge(S["wscale"], 1)
            with act.Fori(0, PAIRS) as p:
                act.wait_ge(S["x_loaded"], p * 32 + 32)
                for h in range(2):
                    act.activation(xin[:, h], xin[:, h], ACT.Abs, scale=LEVELS).then_inc(S["x_abs"], 1)
                for g in range(7):
                    act.wait_ge(S["xt_full"], p * 7 + g + 1)
                    src = ps[:, 6 + g % 2, :].bitcast(BF16)[:, 0:4 * XP].rearrange("p (k y h) -> p k y h", k=4, h=2)
                    dst = xT[:, 1:1 + IMG, 1:1 + IMG].rearrange("p y (h k) -> p k y h", h=2)[:, 4 * g:4 * g + 4]
                    for k in range(4):
                        i = act.activation(dst[:, k], src[:, k], ACT.Copy)
                    i.then_inc(S["xt_ready"], 1)
                for t in range(NW + 3):
                    if t < NW:
                        act.wait_ge(S["conv_full"], p * NW + t + 1)
                        act.activation(x1[:, t], ps[:, 0, 0:ST], ACT.Identity, scale=cscale[:], bias=bconv).then_inc(S["x1_ready"], 1)
                    if 0 <= t - 1 < NW:
                        s = t - 1
                        act.wait_ge(S["xc_ready"], 1 + p * NW + s + 1)
                        act.activation(sq[:, s % 2], xn[:, s], ACT.Square).then_inc(S["sq_ready"], 1)
                    if 0 <= t - 2 < NW:
                        s = t - 2
                        act.wait_ge(S["var_full"], p * NW + s + 1)
                        act.wait_ge(S["rs_ready"], 1 + p * NW + s)
                        act.activation(lnv[:], ps[:, 2, 0:ST], ACT.Ln, bias=epst[:]).then_inc(S["lnv_ready"], 1)
                        act.wait_ge(S["lnv_ready"], 1 + p * NW + s + 1)
                        act.activation(rs[:, s % 2], lnv[:], ACT.Exp, scale=-0.5).then_inc(S["rs_ready"], 1)
                    if 0 <= t - 3 < NW:
                        s = t - 3
                        n = p * NW + s + 1
                        act.wait_ge(S["q_full"], n)
                        act.activation(qH[:, s], ps[:, 3, 0:ST], ACT.Identity, bias=bq).then_inc(S["qH_ready"], 1)
                        act.wait_ge(S["k_full"], n)
                        b = s % 2
                        per = len(range(b, NW, 2))
                        act.wait_ge(ks_stored[b], 1 + p * (192 * per) + 192 * (s // 2))
                        act.activation(kH[:, b], ps[:, 4, 0:ST], ACT.Identity, bias=bk).then_inc(S["kH_ready"], 1)

                with act.Fori(0, NW) as s:
                    T = p * NW + s
                    for t in range(STEPS + 2):
                        if 0 <= t - 2 and t % 2 == 1:
                            w = (t - 2) // 2
                            act.wait_ge(S["u_full"], 1 + T * STEPS + t - 1)
                            act.activation(us[:, :, :, w * RT:w * RT + RT], ps[:, 5, 0:256].rearrange("p (h e t) -> p h e t", h=2, e=2), ACT.Copy).then_inc(S["u_ready"], 1)
                        if 0 <= t - 1 < STEPS:
                            i = t - 1
                            for c in range(2):
                                act.wait_ge(S["st_full"], 1 + (T * STEPS + i) * 2 + c + 1)
                                act.wait_ge(S["u_full"], 1 + T * STEPS + max(i - 1, 0))
                                act.activation(pt[i % 2][:, c], ps[:, 2 + c, :], ACT.Exp, scale=float(HD) ** -0.5).then_inc(S["pt_ready"], 1)
                        if t < STEPS:
                            act.wait_ge(S["mt_full"], 1 + T * STEPS + t + 1)
                            act.wait_ge(S["qb_ready"], 1 + T * STEPS + t + 1)
                            act.activation(qb[t % RING][NP3:NP3 + 1].rearrange("p g h t -> p (g h t)"), ps[NP3:NP3 + 1, 4, :], ACT.Copy).then_inc(S["mt_ready"], 1)
                    for i in range(4):
                        act.wait_ge(S["sum_full"], T * 4 + i + 1)
                        if i >= 2:
                            act.wait_ge(S["un_ready"], T * 4 + i - 1)
                        act.activation(ln_s[:, i % 2], ps[:, i, 0:ST], ACT.Ln).then_inc(S["lns_ready"], 1)
                        act.wait_ge(S["lns_ready"], T * 4 + i + 1)
                        act.activation(rc_s[:, i % 2], ln_s[:, i % 2], ACT.Exp, scale=-1.0).then_inc(S["rcs_ready"], 1)
                    act.wait_ge(S["xc2_ready"], T + 1)
                    act.activation(sq2[:], xc2[:], ACT.Square).then_inc(S["sq2_ready"], 1)
                    act.wait_ge(S["var2_full"], T + 1)
                    act.activation(ln2[:], ps[:, 6, 0:ST], ACT.Ln, bias=epst[:]).then_inc(S["lnv2_ready"], 1)
                    act.wait_ge(S["lnv2_ready"], T + 1)
                    act.activation(rs2[:], ln2[:], ACT.Exp, scale=-0.5).then_inc(S["rs2_ready"], 1)
                    for i in range(4):
                        act.wait_ge(S["h_full"], T * 4 + i + 1)
                        act.activation(hid[:, i], ps[:, i, 0:ST], ACT.Gelu_apprx_tanh, bias=(bm1a, bm1b)[i % 2]).then_inc(S["hid_ready"], 1)
                    load_table(act)

        @block.tensor
        def _(pe):
            for name in 'st_full u_full mt_full'.split():
                pe.sem_inc(S[name], 1)
            pe.wait_ge(S["wabs"], 1)
            pe.matmul(ps[:, 0, 0:1], mean_w[:], wsum[:], start=True, stop=True).then_inc(S["wsum_full"], 1)
            pe.wait_ge(S["wscale"], 1)
            pe.wait_ge(S["sign_ready"], 1)
            with pe.Fori(0, PAIRS) as p:
                pe.wait_ge(S["x_ready"], 1 + p * 2 + 2)
                pe.wait_ge(S["v_ready"], 1 + p * NW)
                for g in range(7):
                    if g >= 2:
                        pe.wait_ge(S["xt_ready"], p * 7 + g - 1)
                    for k in range(4):
                        i = pe.transpose(ps[:, 6 + g % 2, :].bitcast(BF16)[:, k * XP:(k + 1) * XP], xq[:, 4 * g + k, :], identb[0:XP, 0:XP])
                    i.then_inc(S["xt_full"], 1)
                pe.wait_ge(S["xt_ready"], p * 7 + 7)
                for t in range(NW + 3):
                    if t < NW:
                        pe.wait_ge(S["x1_ready"], 1 + p * NW + t)
                        for tap in range(9):
                            dy, dx = tap // 3, tap % 3
                            rhs = xT[:, t * WS + dy:t * WS + dy + WS, dx:dx + IMG].rearrange("p y (n c) -> p n y c", n=NW)
                            i = pe.matmul(ps[:, 0, 0:ST].rearrange("p (n y c) -> p n y c", n=NW, y=WS), wconv[:, tap, :], rhs, start=tap == 0, stop=tap == 8)
                        i.then_inc(S["conv_full"], 1)
                    if 0 <= t - 1 < NW:
                        s = t - 1
                        pe.wait_ge(S["x1_ready"], 1 + p * NW + s + 1)
                        pe.wait_ge(S["xc_ready"], 1 + p * NW + s)
                        pe.matmul(ps[:, 1, 0:ST], mean_w[:], x1[:, s], start=True, stop=True).then_inc(S["mean_full"], 1)
                    if 0 <= t - 2 < NW:
                        s = t - 2
                        pe.wait_ge(S["sq_ready"], p * NW + s + 1)
                        pe.wait_ge(S["lnv_ready"], 1 + p * NW + s)
                        pe.matmul(ps[:, 2, 0:ST], mean_w[:], sq[:, s % 2], start=True, stop=True).then_inc(S["var_full"], 1)
                    if 0 <= t - 3 < NW:
                        s = t - 3
                        n = p * NW + s
                        pe.wait_ge(S["xn_ready"], n + 1)
                        pe.wait_ge(S["qL_ready"], 1 + n)
                        pe.matmul(ps[:, 3, 0:ST], wq[:], xn[:, s], start=True, stop=True).then_inc(S["q_full"], 1)
                        pe.wait_ge(S["kL_ready"], 1 + n)
                        pe.matmul(ps[:, 4, 0:ST], wk[:], xn[:, s], start=True, stop=True).then_inc(S["k_full"], 1)
                        pe.wait_ge(S["v_ready"], 1 + n)
                        for w in range(NW):
                            for d in (0, 64):
                                i = pe.matmul(ps[d:d + 64, 5 + w // 4, 128 * (w % 4):128 * (w % 4) + 128],
                                              xn[:, s, w * RT:w * RT + RT], wv[:], start=True, stop=True)
                        i.then_inc(S["v_full"], 1)
                pe.wait_ge(S["logit_ready"], p * 2 + 1)
                settled(pe)
                for h in range(2):
                    d = slice(64 * h, 64 * h + 64)
                    i = pe.matmul(ps[0:R, h, 0:R], regsum[d, 0, :], regsum[d, 1, :], start=True, stop=True)
                i.then_inc(S["logit_full"], 1)
                pe.wait_ge(S["v_ready"], 1 + p * NW + NW)
                pe.wait_ge(S["logit_ready"], p * 2 + 2)
                settled(pe)

                with pe.Fori(0, NW) as s:
                    T = p * NW + s
                    pe.wait_ge(S["ot_ready"], 1 + T)
                    for t in range(STEPS + 2):
                        if t < STEPS:
                            b = t % RING
                            pe.wait_ge(S["qb_ready"], 1 + T * STEPS + t + 1)

                            pe.wait_ge(S["mx_ready"], 1 + T * STEPS + t)
                            for g in range(NG):
                                for j in range(2):
                                    i = pe.matmul(ps[:, g, 256 * j:256 * j + 256],
                                                  qb[b][:, g, 2 * j:2 * j + 2, :].rearrange("p h t -> p (h t)"),
                                                  kg[b][:, g].rearrange("p k t -> p (k t)"), start=True, stop=True)
                            i.then_inc(S["sm_full"], 1)
                        if t >= 2:
                            i0 = t - 2
                            h, b = i0 % 2, i0 % RING
                            pe.wait_ge(S["vg_ready"], T * STEPS + i0 + 1)
                            pe.wait_ge(S["pt_ready"], 1 + (T * STEPS + i0 + 1) * 2)
                            if h == 0:
                                pe.wait_ge(S["u_ready"], 1 + T * NW + i0 // 2)
                            for c in range(2):
                                for j in range(4):
                                    i = pe.matmul(ps[32 * j:32 * j + 32, 5, 128 * h:128 * h + 128],
                                                  vg[b][:, c * 4 * VC + VC * j:c * 4 * VC + VC * j + 32],
                                                  pt[i0 % 2][:, c, 128 * j:128 * j + 128], start=c == 0, stop=c == 1)
                            i.then_inc(S["u_full"], 1)
                        if 1 <= t <= STEPS:
                            i0 = t - 1
                            b = i0 % RING
                            pe.wait_ge(S["mt_ready"], 1 + T * STEPS + i0 + 1)
                            for c in range(2):
                                pe.wait_ge(S["pt_ready"], 1 + (T * STEPS + i0) * 2)
                                for g in range(NG):
                                    i = pe.matmul(ps[:, 2 + c, 256 * g:256 * g + 256],
                                                  kg[b][:, g, 2 * c:2 * c + 2, :].rearrange("p k t -> p (k t)"),
                                                  qb[b][:, g].rearrange("p h t -> p (h t)"), start=True, stop=True)
                                i.then_inc(S["st_full"], 1)
                        if t < STEPS:
                            pe.wait_ge(S["mx_ready"], 1 + T * STEPS + t + 1)
                            pe.wait_ge(S["mt_ready"], 1 + T * STEPS + t)
                            for j in range(4):
                                i = pe.matmul(ps[NP3:NP3 + 1, 4, 128 * j:128 * j + 128], mx[t % 2][:, j:j + 1], identb[:], start=True, stop=True)
                            i.then_inc(S["mt_full"], 1)
                    pe.wait_ge(S["u_ready"], 1 + T * NW + NW)
                    pe.wait_ge(S["pt_ready"], 1 + (T + 1) * (2 * STEPS))
                    for i in range(4):
                        h, e = i // 2, i % 2
                        pe.matmul(ps[:, i, 0:ST], pick[:], us[:, h, e], start=True, stop=True).then_inc(S["sum_full"], 1)
                    for h in range(2):
                        for e in range(2):
                            pe.wait_ge(S["un_ready"], T * 4 + 2 * h + e + 1)
                            i = pe.matmul(ps[64 * h:64 * h + 64, 4, 0:ST], wo[:, e, :], us[:, h, e], start=e == 0, stop=e == 1)
                    i.then_inc(S["y_full"], 1)
                    pe.wait_ge(S["x2_ready"], T + 1)
                    pe.matmul(ps[:, 5, 0:ST], mean_w[:], x2[:], start=True, stop=True).then_inc(S["mean2_full"], 1)
                    pe.wait_ge(S["sq2_ready"], T + 1)
                    pe.matmul(ps[:, 6, 0:ST], mean_w[:], sq2[:], start=True, stop=True).then_inc(S["var2_full"], 1)
                    pe.wait_ge(S["xn2_ready"], T + 1)
                    for h in range(2):
                        for m in range(2):
                            pe.matmul(ps[:, 2 * h + m, 0:ST], w1[:, h, 128 * m:128 * m + 128], xn2[:], start=True, stop=True).then_inc(S["h_full"], 1)
                    for h in range(2):
                        for m in range(2):
                            pe.wait_ge(S["hid_ready"], T * 4 + 2 * h + m + 1)
                            i = pe.matmul(ps[64 * h:64 * h + 64, 4, 0:ST], w2[:, m, :], hid[:, 2 * h + m], start=m == 0, stop=m == 1)
                    i.then_inc(S["o_full"], 1)
                    pe.wait_ge(S["x3_ready"], T + 1)
                    for t in range(4):
                        i = pe.transpose(ps[0:OT, 5, 128 * t:128 * t + 128], x3[:, OT * t:OT * t + OT], ident[:])
                    i.then_inc(S["t_full"], 1)


WEIGHT_DMAS = 12 + 16 + 1 + 4 + 8

_INS = ["x", "L0_conv_W", "L0_conv_b", "L1_conv_ln1_g", "L1_conv_ln1_b", "L1_conv_wqkv", "L1_conv_bqkv",
        "L1_conv_wo", "L1_conv_bo", "L1_conv_ln2_g", "L1_conv_ln2_b", "L1_conv_w1", "L1_conv_bm1",
        "L1_conv_w2", "L1_conv_bm2"]


def kernel(**inputs):
    import numpy as _np
    import concourse.bacc as _bacc
    from concourse import mybir as _mybir
    from concourse.bass_utils import run_bass_kernel_spmd as _run

    nc = _bacc.Bacc("TRN2", target_bir_lowering=False, num_devices=1)
    arrays, io = {}, {}
    for name in _INS:
        a = _np.ascontiguousarray(inputs[name])
        arrays[f"in_{name}"] = a
        io[name] = nc.dram_tensor(f"in_{name}", a.shape, _mybir.dt.from_np(a.dtype), kind="ExternalInput").ap()
    io["out"] = nc.dram_tensor("out_0", inputs["x"].shape, _mybir.dt.float32, kind="ExternalOutput").ap()
    build(nc, io)
    r = _run(nc, [arrays], core_ids=[0])
    return r.results[0]["out_0"]
```

```python
from contextlib import ExitStack

import concourse.bass as bass
from concourse import mybir
from concourse.alu_op_type import AluOpType as ALU

ACT = mybir.ActivationFunctionType
AX = mybir.AxisListType
F32 = mybir.dt.float32
F32R = mybir.dt.float32r
BF16 = mybir.dt.bfloat16
U32 = mybir.dt.uint32

C = 64
IMG = 56
NW = 7
WS = IMG // NW
R = NW * NW
RT = WS * WS
ST = NW * RT
HEADS = 8
HD = C // HEADS
TOPK = 4
KEYS = TOPK * RT
PADW = IMG + 2
XP = 2 * IMG
XK = IMG // 2
RND = 12582912.0
LEVELS = 7.0
EPS = 1e-5
HG = 4
NG = HEADS // HG
QR = HG * HD
NP3 = 3 * QR
VC = 17
RING = 4
STEPS = 2 * NW
OT = ST // 4
HALF = 4
POOL_STEPS = (1, 5, 6, 7, 8, 11, 12)
LATE = (1, 12, 13)
SLOT = [0, 1, 2, 3, 0, 1, 2, 3, 0, 1, 2, 0, 1, 2]


def slot_age(i):
    return next(j for j in range(1, STEPS + 1) if SLOT[(i - j) % STEPS] == SLOT[i])


def by_pool(n):
    return len([i for i in POOL_STEPS if i < n])


def back(i, n, first):
    return max(i - n, 0) if first else i - n


def here(i, kind):
    return kind != "end" if i >= 0 else kind != "first"


def region_copied(t, kind):
    if t == 1:
        return [-1] if kind != "first" else []
    if kind == "end":
        return []
    return [(t - 3) // 2] if t % 2 else []


def build(nc, io):
    x, out = io["x"], io["out"]
    PAIRS = x.shape[0] // 2
    with ExitStack() as ctx:
        def sb(name, shape, dt=F32):
            return ctx.enter_context(nc.sbuf_tensor(name, shape, dt))

        def sem(name):
            return ctx.enter_context(nc.semaphore(name))

        ident = sb("ident", [128, 128])
        identb = sb("identb", [128, 128], BF16)
        pick = sb("pick", [128, 128])
        headmask3 = sb("headmask3", [128, 3, HG])
        headmask = sb("headmask", [128, HG])
        mean_w = sb("mean_w", [128, 128])
        center_w = sb("center_w", [128, 128])
        wq = sb("wq", [128, 128])
        wk = sb("wk", [128, 128])
        wv = sb("wv", [128, 128])
        w1 = sb("w1", [128, 2, 4 * C])
        w2 = sb("w2", [128, 2, C])
        wo = sb("wo", [128, 2, C])
        wconv = sb("wconv", [128, 9, 128], BF16)
        wsum = sb("wsum", [128, 1])
        cscale = sb("cscale", [128, 1])
        cols = sb("cols", [128, 12])
        bvb = sb("bvb", [128, 2 * C])
        bm2b = sb("bm2b", [128, C])
        epst = sb("epst", [128, 1])
        zero = sb("zero", [128, 1])
        bconv, g1, b1, g2, b2, bq, bk, bo, bm1a, bm1b = (cols[:, i:i + 1] for i in range(10))

        xin_ = sb("xin", [128, 2 * XK * C])
        xin = xin_[0:XP].rearrange("p (h k c) -> p h k c", h=2, c=C)
        hid_ = sb("hid", [128, 4 * ST])
        xT = sb("xT", [128, PADW, PADW], BF16)
        x1 = sb("x1", [128, NW, ST])
        xn = sb("xn", [128, NW, ST])
        sq = sb("sq", [128, 2, ST])
        wconv_f = sq[:].rearrange("p m b -> p (m b)")[:, 0:9 * C].rearrange("p (m b) -> p m b", b=C)
        lnv = sb("lnv", [128, ST])
        rs = sb("rs", [128, 2, ST])
        qH = sb("qH", [128, NW, ST], F32R)
        qL = sb("qL", [128, NW, ST], F32R)
        k_ = sb("k_", [128, 4, ST])
        kH, kL = k_[:, 0:2].bitcast(F32R), k_[:, 2:4].bitcast(F32R)
        regsum = sb("regsum", [128, 2, R])
        ks_ = [sb(f"ks{i}", [128, R, NG * RT], F32R) for i in range(2)]
        ks = [t[0:NP3] for t in ks_]
        xq = ks_[0][0:XP].rearrange("p y t -> p (y t)")[:, 0:XK * C].bitcast(BF16).rearrange("p (k n) -> p k n", k=XK)
        vs = sb("vs", [128, R, 2, 4 * VC])
        lg = sb("lg", [R, 2, R])
        top = sb("top", [R, 2, 8])
        topi = sb("topi", [R, 2, 8], U32)
        idx = sb("idx", [1, 2 * R * TOPK], U32)
        idx_dram = nc.dram_tensor("idx_scratch", [2, R, TOPK], U32, kind="Internal").ap()

        qs = [sb(f"qs{i}", [128, NG, ST], F32R) for i in range(2)]
        kg = [sb(f"kg{i}", [128, NG, TOPK, RT], F32R) for i in range(RING)]
        vg = [sb(f"vg{i}", [128, 2 * 4 * VC + 16]) for i in range(RING)]
        qb = [sb(f"qb{i}", [128, NG, HG, RT], F32R) for i in range(RING)]
        mx = [sb(f"mx{i}", [128, 4], BF16) for i in range(2)]
        pt = [xin_[:, 1024 * i:1024 * i + 1024].rearrange("p (c n) -> p c n", c=2) for i in range(2)]
        wpos, wneg = (xin_[:, 1024 * i:1024 * i + 9 * C].rearrange("p (m b) -> p m b", b=C) for i in range(2))
        x3 = sq[:, 0]
        ot = rs[0:OT].rearrange("p m b -> p (m b)")[:, 0:512].rearrange("p (h t c) -> p h t c", h=2, c=C)
        hid = hid_[:].rearrange("p (m t) -> p m t", m=4)
        us = k_[:].rearrange("p (h e) t -> p h e t", h=2)
        aside = hid_[:, 0:512].rearrange("p (h e t) -> p h e t", h=2, e=2)
        rc_s = [sq[:, 0], sq[:, 1], rs[:, 0], rs[:, 1]]
        un = xn[:, 0:4].rearrange("p (h e) t -> p h e t", h=2)
        x2, nm2, st2 = (xn[:, i] for i in range(4, 7))

        ps = ctx.enter_context(nc.psum_tensor("ps", [128, 8, 512], F32))

        names = """w_loaded zeroed const_ready diag_ready wabs wsum_full wscale sign_ready zero2
            x_loaded x_abs x_rounded x_ready xt_full xt_ready
            conv_full x1_ready mean_full xc_ready sq_ready var_full lnv_ready rs_ready xh_ready xn_ready
            q_full qH_ready qL_ready k_full kH_ready kL_ready v_full v_ready
            logit_full logit_ready top_ready topi_ready idx_stored idx_loaded qs_ready
            qb_ready qc_ready z_ready vg_ready sm_full mx_ready mt_full mt_ready st_full pt_ready u_full u_ready
            sum_full lns_ready rcs_ready un_ready y_full x2_ready xc2_full sq2_ready
            var2_full lnv2_ready rs2_ready xh2_ready xn2_ready h_full hid_ready o_full x3_ready
            t_full ot_ready out_stored waited qs_late_ready""".split()
        S = {n: sem(n) for n in names}
        ks_stored = [sem("ks_stored0"), sem("ks_stored1")]
        kl_stored = [sem("kl_stored0"), sem("kl_stored1")]

        tables = []
        block = ctx.enter_context(nc.Block())

        def chosen(eng, regs, s, i):
            at = (s * STEPS + i) * TOPK
            eng.load(regs, idx[0:1, bass.ds(at, TOPK)])
            return [eng.snap(r, min_val=0, max_val=R - 1) for r in regs]

        def settled(eng):
            eng.sem_inc(S["waited"], 1)

        def load_table(act):
            act.add_instruction(mybir.InstLoadActFuncSet(name=f"I-{4000000 + len(tables)}", act_func_set_id=6, engine=mybir.EngineType.Activation, ins=[], outs=[]))
            tables.append(1)

        @block.sync
        def _(sp):
            for name in 'out_stored'.split():
                sp.sem_inc(S[name], 1)
            for t in ks_stored:
                sp.sem_inc(t, 1)
            n = [0]
            def query_stack(s, part):
                first, last = (0, HALF) if part == "qs_ready" else (HALF, NW)
                cut = slice(first * RT, last * RT)
                for h in range(2):
                    for g in range(NG):
                        rows = slice(64 * h + QR * g, 64 * h + QR * g + QR)
                        for q, src in enumerate((qH, qH, qL)):
                            sp.dma_start(qs[h][QR * q:QR * q + QR, g, cut].bitcast(F32),
                                         src[rows, bass.ds(s, 1), cut].bitcast(F32).rearrange("p o t -> p (o t)")).then_inc(S[part], 16)

            def load_x(pair):
                for h in range(2):
                    sp.dma_start(xin[:, h], x[bass.ds(pair * 2 + h, 1)].rearrange("o (p y) (h c) k -> (o p y h) c k", y=1, h=2)).then_inc(S["x_loaded"], 16)

            def attend(p, s, kind):
                T = p * NW + s
                if kind != "end":
                    sp.wait_ge(S["qb_ready"], 1 + T * STEPS)
                    settled(sp)
                    sp.wait_ge(S["qc_ready"], 1 + T * len(POOL_STEPS))
                    query_stack(s, "qs_late_ready")
                if kind in ("first", "middle"):
                    sp.wait_ge(S["qb_ready"], 1 + T * STEPS + 2 * HALF)
                    settled(sp)
                    sp.wait_ge(S["qc_ready"], 1 + T * len(POOL_STEPS) + by_pool(2 * HALF))
                    query_stack(s + 1, "qs_ready")
                if kind == "end":
                    sp.wait_ge(S["u_full"], 1 + T * STEPS)
                    settled(sp)
                    load_x((p + 1) % PAIRS)
                if kind != "first":
                    sp.wait_ge(S["ot_ready"], 1 + T)
                    for h in range(2):
                        dst = out[bass.ds(p * 2 + h, 1), bass.ds((s - 1) * WS, WS)].rearrange("o y c k -> (o y c k)")
                        sp.dma_start(dst.rearrange("(p n) -> p n", p=OT), ot[:, h].rearrange("p t c -> p (t c)")).then_inc(S["out_stored"], 16)

            def load(dst, src):
                sp.dma_start(dst, src).then_inc(S["w_loaded"], 16)
                n[0] += 1

            def col(i, src):
                for h in range(2):
                    load(cols[64 * h:64 * h + 64, i:i + 1], src.rearrange("(p o) -> p o", o=1))

            sp.wait_ge(S["zeroed"], 1)
            W = io["L0_conv_W"].rearrange("m b i o -> i (m b) o")
            for h in range(2):
                load(wconv_f[64 * h:64 * h + 64], W)
                d = slice(64 * h, 64 * h + 64)
                load(wq[d, d], io["L1_conv_wqkv"][:, 0:C])
                load(wk[d, d], io["L1_conv_wqkv"][:, C:2 * C])
                load(wv[d, d], io["L1_conv_wqkv"][:, 2 * C:3 * C])
                load(w1[d, h, :], io["L1_conv_w1"])
                load(bvb[:, d], io["L1_conv_bqkv"][2 * C:3 * C].rearrange("(o n) -> o n", o=1).broadcast_to([128, C]))
            col(0, io["L0_conv_b"])
            col(1, io["L1_conv_ln1_g"])
            col(2, io["L1_conv_ln1_b"])
            col(3, io["L1_conv_ln2_g"])
            col(4, io["L1_conv_ln2_b"])
            col(5, io["L1_conv_bqkv"][0:C])
            col(6, io["L1_conv_bqkv"][C:2 * C])
            col(7, io["L1_conv_bo"])
            load(bm2b[:], io["L1_conv_bm2"].rearrange("(o n) -> o n", o=1).broadcast_to([128, C]))
            for m in range(2):
                load(cols[:, 8 + m:9 + m], io["L1_conv_bm1"][128 * m:128 * m + 128].rearrange("(p o) -> p o", o=1))
                load(w2[:, m, :], io["L1_conv_w2"][128 * m:128 * m + 128, :])
            for j in range(4):
                for e in range(2):
                    load(wo[32 * j + 8 * e:32 * j + 8 * e + 8, e, :], io["L1_conv_wo"][16 * j + 8 * e:16 * j + 8 * e + 8, :])
            assert n[0] == WEIGHT_DMAS

            sp.wait_ge(S["sign_ready"], 1)
            load_x(0)
            with sp.Fori(0, PAIRS) as p:
                for s in range(NW):
                    sp.wait_ge(S["kL_ready"], 1 + p * NW + s + 1)
                    for h in range(2):
                        for g in range(NG):
                            rows = slice(64 * h + QR * g, 64 * h + QR * g + QR)
                            for q, src in enumerate((kH, kL, kH)):
                                if q == 1:
                                    continue
                                sp.dma_start(ks[h][QR * q:QR * q + QR, s * NW:s * NW + NW, g * RT:g * RT + RT].bitcast(F32),
                                             src[rows, s % 2, :].bitcast(F32).rearrange("p (n t) -> p n t", n=NW)).then_inc(ks_stored[s % 2], 16)
                    if s == 1:
                        sp.wait_ge(S["qb_ready"], 1 + p * (NW * STEPS))
                        settled(sp)
                        sp.wait_ge(S["qc_ready"], 1 + p * (NW * len(POOL_STEPS)))
                        query_stack(0, "qs_ready")
                sp.wait_ge(S["topi_ready"], p + 1)
                sp.dma_start(idx[0:1, :].rearrange("o (y h k) -> o y h k", h=2, k=TOPK), topi[:, :, 0:TOPK]).then_inc(S["idx_loaded"], 16)
                sp.wait_ge(S["idx_loaded"], p * 16 + 16)
                for b in range(2):
                    sp.wait_ge(ks_stored[b], 1 + (p + 1) * (128 * len(range(b, NW, 2))))
                attend(p, 0, "first")
                with sp.Fori(1, NW - 1) as s:
                    attend(p, s, "middle")
                attend(p, NW - 1, "last")
                attend(p, NW, "end")
            sp.wait_ge(S["out_stored"], 1 + 32 * PAIRS * NW)

        @block.gpsimd
        def _(pool):
            for name in 'qc_ready vg_ready'.split():
                pool.sem_inc(S[name], 1)
            Z = S["zero2"]
            for i, t in enumerate((ident, pick, headmask3)):
                pool.memset(t[:], 1.0 if t is headmask3 else 0.0).then_inc(Z, 1)
            pool.wait_ge(Z, 3)
            pool.affine_select(out=ident[:], in_=ident[:], compare_op=ALU.not_equal, fill=1.0, base=0,
                               pattern=[[-1, 128]], channel_multiplier=1).then_inc(Z, 1)
            v = pick[:].rearrange("p (m b) -> p m b", m=4)
            pool.affine_select(out=v, in_=v, compare_op=ALU.not_equal, fill=1.0, base=-16,
                               pattern=[[-32, 4], [0, 32]], channel_multiplier=1).then_inc(Z, 1)
            pool.affine_select(out=headmask3[:], in_=headmask3[:], compare_op=ALU.is_ge, fill=0.0, base=0,
                               pattern=[[-QR, 3], [-HD, HG]], channel_multiplier=1).then_inc(Z, 1)
            pool.wait_ge(Z, 6)
            pool.affine_select(out=headmask3[:], in_=headmask3[:], compare_op=ALU.is_ge, fill=0.0, base=HD - 1,
                               pattern=[[QR, 3], [HD, HG]], channel_multiplier=-1).then_inc(S["const_ready"], 1)
            pool_regs = [pool.alloc_register(f"pool_region{k}") for k in range(TOPK)]

            def queries(p, s, i, first):
                T = p * NW + s
                pool.wait_ge(S["st_full"], 1 + (T * STEPS + back(i, slot_age(i) - 1, first)) * 2)
                pool.wait_ge(S["vg_ready"], 1 + T * STEPS + i)
                pool.wait_ge(S["qs_ready"], (T + 1) * (16 * 12))
                if i >= 2 * HALF:
                    pool.wait_ge(S["qs_late_ready"], (T + 1) * (16 * 12))
                settled(pool)
                q = qs[i % 2][:, 1, (i // 2) * RT:(i // 2) * RT + RT].bitcast(F32)
                pool.tensor_tensor(qb[SLOT[i]][:, 1],
                                   q.unsqueeze(1).broadcast_to([128, HG, RT]),
                                   headmask[:].unsqueeze(2).broadcast_to([128, HG, RT]), ALU.mult).then_inc(S["qc_ready"], 1)

            def values(p, s, i, first):
                T = p * NW + s
                pool.wait_ge(S["u_full"], 1 + T * STEPS + back(i, slot_age(i) - 1, first))
                pool.wait_ge(S["qc_ready"], 1 + T * len(POOL_STEPS) + by_pool(i + 1))
                settled(pool)
                for k, region in enumerate(chosen(pool, pool_regs, s, i)):
                    rows = slice(64 * (k % 2), 64 * (k % 2) + 64)
                    j = pool.tensor_copy(vg[SLOT[i]][rows, (k // 2) * 4 * VC:(k // 2 + 1) * 4 * VC],
                                         vs[rows, bass.ds(region, 1), i % 2, :].rearrange("p o n -> p (o n)"))
                j.then_inc(S["vg_ready"], 1)

            with pool.Fori(0, PAIRS) as p:
                for s in range(NW):
                    pool.wait_ge(S["kL_ready"], 1 + p * NW + s + 1)
                    settled(pool)
                    for h in range(2):
                        for g in range(NG):
                            pool.dma_start(ks[h][QR:2 * QR, s * NW:s * NW + NW, g * RT:g * RT + RT].bitcast(F32),
                                           kL[64 * h + QR * g:64 * h + QR * g + QR, s % 2, :].bitcast(F32).rearrange("p (n t) -> p n t", n=NW)).then_inc(kl_stored[s % 2], 16)
                pool.wait_ge(S["v_ready"], 1 + p * NW + NW)
                pool.wait_ge(S["idx_loaded"], p * 16 + 16)
                settled(pool)
                for i in range(STEPS):
                    if i in POOL_STEPS:
                        queries(p, 0, i, True)
                    values(p, 0, i, True)
                with pool.Fori(1, NW) as s:
                    for i in range(STEPS):
                        if i in POOL_STEPS:
                            queries(p, s, i, False)
                        values(p, s, i, False)

        @block.vector
        def _(v):
            for name in 'x_ready xc_ready qL_ready kL_ready v_ready qb_ready mx_ready ot_ready'.split():
                v.sem_inc(S[name], 1)
            ch = [0]
            v_regs = [v.alloc_register(f"v_region{k}") for k in range(TOPK)]

            def link(ins):
                ch[0] += 1
                ins.then_inc(S["diag_ready"], 1)
                v.wait_ge(S["diag_ready"], ch[0])

            for t in (wq, wk, wv, w1, wo, mean_w):
                v.memset(t[:], 0.0)
            v.memset(zero[:], 0.0)
            v.memset(epst[:], EPS)
            v.memset(wconv[:], 0.0)
            v.memset(xT[:], 0.0)
            v.memset(vs[:], 1.0)
            for t in kg:
                v.memset(t[:].bitcast(F32), -1.0)
            for t in vg:
                v.memset(t[:], 1.0)
            for t in qs:
                v.memset(t[NP3:128].bitcast(F32), 0.0)
            link(v.memset(mx[0][:], 0.0))
            v.memset(mean_w[0:64, 0:64], 1.0 / C)
            v.memset(mean_w[64:128, 64:128], 1.0 / C).then_inc(S["zeroed"], 1)
            v.wait_ge(S["const_ready"], 1)
            v.tensor_copy(identb[:], ident[:])
            v.wait_ge(S["zeroed"], 1)
            v.tensor_tensor(center_w[:], ident[:], mean_w[:], ALU.subtract)
            link(v.tensor_reduce(headmask[:], headmask3[:].rearrange("p m b -> p b m"), AX.X, ALU.add))
            v.wait_ge(S["w_loaded"], 16 * WEIGHT_DMAS)
            v.tensor_reduce(wsum[:], wconv_f[:].rearrange("p m b -> p (m b)"), AX.X, ALU.add, apply_absolute_value=True).then_inc(S["wabs"], 1)
            v.tensor_scalar(wpos[:], wconv_f[:], 0.0, None, ALU.is_gt)
            link(v.tensor_scalar(wneg[:], wconv_f[:], 0.0, None, ALU.is_lt))
            for h in range(2):
                d = slice(64 * h, 64 * h + 64)
                i = v.tensor_tensor(wconv[d, :, d], wpos[d], wneg[d], ALU.subtract)
            i.then_inc(S["sign_ready"], 1)
            v.wait_ge(S["wsum_full"], 1)
            v.tensor_scalar(cscale[:], ps[:, 0, 0:1], 1.0 / (9 * C), 1.0 / LEVELS, ALU.mult, ALU.mult).then_inc(S["wscale"], 1)

            def queries(p, s, i, first):
                T = p * NW + s
                v.wait_ge(S["st_full"], 1 + (T * STEPS + back(i, slot_age(i) - 1, first)) * 2)
                if i == 0:
                    v.wait_ge(S["qs_ready"], (T + 1) * (16 * 12))
                if i == 2 * HALF:
                    v.wait_ge(S["qs_late_ready"], (T + 1) * (16 * 12))
                q = qs[i % 2][:, :, (i // 2) * RT:(i // 2) * RT + RT].bitcast(F32)
                for g in range(1 if i in POOL_STEPS else NG):
                    v.tensor_tensor(qb[SLOT[i]][:, g],
                                    q[:, g].unsqueeze(1).broadcast_to([128, HG, RT]),
                                    headmask[:].unsqueeze(2).broadcast_to([128, HG, RT]), ALU.mult)
                for k, region in enumerate(chosen(v, v_regs, s, i)):
                    j = v.tensor_copy(kg[SLOT[i]][0:NP3, :, k, :],
                                      ks[i % 2][:, bass.ds(region, 1), :].rearrange("p o (g t) -> p (o g) t", g=NG))
                j.then_inc(S["qb_ready"], 1)

            def finish_first(p, s, t):
                U = p * NW + s
                if t == 9:
                    v.wait_ge(S["rs2_ready"], U + 1)
                    v.tensor_tensor(nm2[:], ps[:, 7, 0:ST], st2[:], ALU.mult).then_inc(S["xh2_ready"], 1)
                    v.wait_ge(S["xh2_ready"], U + 1)
                    v.tensor_scalar(nm2[:], nm2[:], g2, b2, ALU.mult, ALU.add).then_inc(S["xn2_ready"], 1)

                if t == 13:
                    v.wait_ge(S["o_full"], U + 1)
                    for h in range(2):
                        def halves(t):
                            return t.rearrange("p (n y h t) -> p n y h t", n=NW, y=WS, h=2)[:, :, :, h, :]
                        i = v.tensor_tensor(x3[:].rearrange("p (t y n h) -> p n y h t", t=4, y=WS, n=NW)[:, :, :, h, :],
                                            halves(ps[:, 6, 0:ST]), halves(x2[:]), ALU.add)
                    i.then_inc(S["x3_ready"], 1)

            def finish(p, s, t):
                U = p * NW + s
                for i in {3: (0, 1), 4: (2,), 5: (3,)}.get(t, ()):
                    v.wait_ge(S["rcs_ready"], U * 4 + i + 1)
                    v.tensor_tensor(un[:, i // 2, i % 2], us[:, i // 2, i % 2], rc_s[i], ALU.mult).then_inc(S["un_ready"], 1)
                if t == 6:
                    v.wait_ge(S["y_full"], U + 1)
                    v.scalar_tensor_tensor(x2[:], ps[:, 6, 0:ST], bo, x1[:, bass.ds(s, 1), :].rearrange("p o t -> p (o t)"), ALU.add, ALU.add).then_inc(S["x2_ready"], 1)
                if t == 10:
                    for m in range(2):
                        v.wait_ge(S["h_full"], U * 4 + m + 1)
                        v.tensor_copy(hid[:, m], ps[:, 6 + m, 0:ST]).then_inc(S["z_ready"], 1)
                if t == 13:
                    v.wait_ge(S["t_full"], U + 1)
                    v.wait_ge(S["out_stored"], 1 + U * 32)
                    for h in range(2):
                        i = v.tensor_tensor(ot[:, h], ps[0:OT, 7, :].rearrange("p (t h c) -> p h t c", t=4, h=2)[:, h],
                                            bm2b[0:OT].unsqueeze(1).broadcast_to([OT, 4, C]), ALU.add)
                    i.then_inc(S["ot_ready"], 1)

            def attend(p, s, kind):
                T = p * NW + s
                for t in range(STEPS):
                    if kind != "end":
                        v.wait_ge(S["sm_full"], T * STEPS + t + 1)
                        v.wait_ge(S["mt_full"], 1 + T * STEPS + back(t, 1, kind == "first"))
                        v.tensor_reduce(mx[t % 2][:].rearrange("p (g j) -> p g j", g=2),
                                        ps[:, 0:2, :].rearrange("p g (j k) -> p g j k", j=2), AX.X, ALU.max).then_inc(S["mx_ready"], 1)
                    if kind != "first":
                        finish_first(p, s - 1, t)
                    if kind != "end":
                        if t + 2 < STEPS:
                            queries(p, s, t + 2, kind == "first")
                        elif kind != "last":
                            queries(p, s + 1, t + 2 - STEPS, False)
                    if kind != "first":
                        finish(p, s - 1, t)
                    if kind == "end":
                        prepare(p + 1, t)

            def prepare(n, t):
                if 5 <= t < 9:
                    h = (t - 5) // 2
                    if t % 2:
                        v.wait_ge(S["x_abs"], n * 2 + h + 1)
                        v.tensor_scalar(xin[:, h], xin[:, h], LEVELS, RND, ALU.min, ALU.add).then_inc(S["x_rounded"], 1)
                    else:
                        v.wait_ge(S["x_rounded"], n * 2 + h + 1)
                        v.tensor_scalar(xq[:, :, C * h:C * h + C], xin[:, h], RND, None, ALU.subtract).then_inc(S["x_ready"], 1)

            for t in range(STEPS):
                prepare(0, t)
            with v.Fori(0, PAIRS) as p:
                for t in range(NW + 3):
                    if 0 <= t - 1 < NW:
                        s = t - 1
                        v.wait_ge(S["mean_full"], p * NW + s + 1)
                        v.tensor_tensor(xn[:, s], x1[:, s], ps[:, 1, 0:ST], ALU.subtract).then_inc(S["xc_ready"], 1)
                    if 0 <= t - 2 < NW:
                        s = t - 2
                        v.wait_ge(S["rs_ready"], 1 + p * NW + s + 1)
                        v.tensor_tensor(xn[:, s], xn[:, s], rs[:, s % 2], ALU.mult).then_inc(S["xh_ready"], 1)
                        v.wait_ge(S["xh_ready"], p * NW + s + 1)
                        v.tensor_scalar(xn[:, s], xn[:, s], g1, b1, ALU.mult, ALU.add).then_inc(S["xn_ready"], 1)
                    if 0 <= t - 3 < NW:
                        s = t - 3
                        n = p * NW + s + 1
                        v.wait_ge(S["qH_ready"], n)
                        v.tensor_reduce(regsum[:, 0, s * NW:s * NW + NW], ps[:, 3, 0:ST].rearrange("p (n t) -> p n t", n=NW), AX.X, ALU.add)
                        v.scalar_tensor_tensor(qL[:, s], ps[:, 3, 0:ST], bq, qH[:, s].bitcast(F32), ALU.add, ALU.subtract).then_inc(S["qL_ready"], 1)
                        v.wait_ge(S["kH_ready"], n)
                        v.tensor_reduce(regsum[:, 1, s * NW:s * NW + NW], ps[:, 4, 0:ST].rearrange("p (n t) -> p n t", n=NW), AX.X, ALU.add)
                        v.scalar_tensor_tensor(kL[:, s % 2], ps[:, 4, 0:ST], bk, kH[:, s % 2].bitcast(F32), ALU.add, ALU.subtract).then_inc(S["kL_ready"], 1)
                        v.wait_ge(S["v_full"], n)
                        for b, r0, nr in ((5, 0, 4), (6, 4, 3)):
                            i = v.tensor_tensor(
                                vs[:, s * NW + r0:s * NW + r0 + nr].rearrange("p y h (j c) -> p y (h j) c", c=VC)[:, :, :, 0:16],
                                ps[:, b, 0:128 * nr].rearrange("p (y j c) -> p y j c", y=nr, c=16),
                                bvb[:].rearrange("p (j c) -> p j c", c=16).unsqueeze(1).broadcast_to([128, nr, 8, 16]), ALU.add)
                        i.then_inc(S["v_ready"], 1)
                v.wait_ge(S["kL_ready"], 1 + p * NW + NW)
                v.scalar_tensor_tensor(regsum[:, 0], bq.broadcast_to([128, R]), float(RT), regsum[:, 0], ALU.mult, ALU.add)
                v.scalar_tensor_tensor(regsum[:, 1], bk.broadcast_to([128, R]), float(RT), regsum[:, 1], ALU.mult, ALU.add).then_inc(S["logit_ready"], 1)
                v.wait_ge(S["logit_full"], p + 1)
                v.tensor_copy(lg[:], ps[0:R, 0:2, 0:R]).then_inc(S["logit_ready"], 1)
                v.wait_ge(S["logit_ready"], p * 2 + 2)
                settled(v)
                for h in range(2):
                    v.max(top[:, h], lg[:, h]).then_inc(S["top_ready"], 1)
                v.wait_ge(S["top_ready"], p * 2 + 2)
                settled(v)
                for h in range(2):
                    i = v.max_index(topi[:, h], top[:, h], lg[:, h])
                i.then_inc(S["topi_ready"], 1)
                v.wait_ge(S["idx_loaded"], p * 16 + 16)
                for b in range(2):
                    v.wait_ge(ks_stored[b], 1 + (p + 1) * (128 * len(range(b, NW, 2))))
                    v.wait_ge(kl_stored[b], (p + 1) * (64 * len(range(b, NW, 2))))
                settled(v)

                queries(p, 0, 0, True)
                queries(p, 0, 1, True)
                attend(p, 0, "first")
                with v.Fori(1, NW - 1) as s:
                    attend(p, s, "middle")
                attend(p, NW - 1, "last")
                attend(p, NW, "end")

        @block.scalar
        def _(act):
            for name in 'x1_ready lnv_ready rs_ready u_ready pt_ready mt_ready'.split():
                act.sem_inc(S[name], 1)
            load_table(act)

            def finish(p, s, t):
                U = p * NW + s
                for i in {2: (0, 1), 3: (2,), 4: (3,)}.get(t, ()):
                    act.wait_ge(S["sum_full"], U * 4 + i + 1)
                    if i == 2:
                        act.wait_ge(S["out_stored"], 1 + U * 32)
                    act.activation(rc_s[i], ps[:, 6 + i % 2, 0:ST], ACT.Ln).then_inc(S["lns_ready"], 1)
                    act.wait_ge(S["lns_ready"], U * 4 + i + 1)
                    act.activation(rc_s[i], rc_s[i], ACT.Exp, scale=-1.0).then_inc(S["rcs_ready"], 1)
                if t == 7:
                    act.wait_ge(S["xc2_full"], U + 1)
                    act.activation(st2[:], ps[:, 7, 0:ST], ACT.Square).then_inc(S["sq2_ready"], 1)
                if t == 8:
                    act.wait_ge(S["var2_full"], U + 1)
                    act.activation(st2[:], ps[:, 6, 0:ST], ACT.Ln, bias=epst[:]).then_inc(S["lnv2_ready"], 1)
                    act.wait_ge(S["lnv2_ready"], U + 1)
                    act.activation(st2[:], st2[:], ACT.Exp, scale=-0.5).then_inc(S["rs2_ready"], 1)
                if t == 11:
                    for i in (2, 3, 0, 1):
                        if i < 2:
                            act.wait_ge(S["z_ready"], U * 2 + i + 1)
                        else:
                            act.wait_ge(S["h_full"], U * 4 + i + 1)
                        src = hid[:, i] if i < 2 else ps[:, 4 + i, 0:ST]
                        act.activation(hid[:, i], src, ACT.Gelu_apprx_tanh, bias=(bm1a, bm1b)[i % 2]).then_inc(S["hid_ready"], 1)
                    load_table(act)

            def attend(p, s, kind):
                T = p * NW + s
                G = T * STEPS
                for t in range(STEPS):
                    if kind == "end":
                        prepare(p + 1, t)
                    if t == 7 and kind != "end":
                        if kind != "first":
                            act.wait_ge(S["un_ready"], T * 4)
                        act.wait_ge(S["u_ready"], 1 + T * NW + 2)
                        act.activation(us[:, :, :, 0:2 * RT], aside, ACT.Copy)
                    for n in region_copied(t, kind):
                        act.wait_ge(S["u_full"], 1 + G + 2 * n + 2)
                        cut = slice((n % NW) * RT, (n % NW) * RT + RT)
                        dst = aside[:, :, :, cut] if n in (0, 1) else us[:, :, :, cut]
                        act.activation(dst, ps[:, 5, 0:256].rearrange("p (h e t) -> p h e t", h=2, e=2), ACT.Copy).then_inc(S["u_ready"], 1)
                    if here(t - 1, kind):
                        i = t - 1
                        for c in range(2):
                            act.wait_ge(S["st_full"], 1 + (G + i) * 2 + c + 1)
                            act.wait_ge(S["u_full"], 1 + G + back(i, 1, kind == "first"))
                            act.activation(pt[i % 2][:, c], ps[:, 2 + c, :], ACT.Exp, scale=float(HD) ** -0.5).then_inc(S["pt_ready"], 1)
                    if kind != "end":
                        act.wait_ge(S["mt_full"], 1 + G + t + 1)
                        act.wait_ge(S["qb_ready"], 1 + G + t + 1)
                        act.wait_ge(S["qc_ready"], 1 + T * len(POOL_STEPS) + by_pool(t + 1))
                        act.activation(qb[SLOT[t]][NP3:NP3 + 1].rearrange("p g h t -> p (g h t)"), ps[NP3:NP3 + 1, 4, :], ACT.Copy).then_inc(S["mt_ready"], 1)
                    if kind != "first":
                        finish(p, s - 1, t)

            def prepare(n, t):
                if t in (4, 5):
                    act.wait_ge(S["x_loaded"], n * 32 + 32)
                    act.activation(xin[:, t - 4], xin[:, t - 4], ACT.Abs, scale=LEVELS).then_inc(S["x_abs"], 1)
                for g in {10: (0,), 11: (1,), 12: (2, 3), 13: (4, 5, 6)}.get(t, ()):
                    act.wait_ge(S["xt_full"], n * 7 + g + 1)
                    src = ps[:, g % 2, :].bitcast(BF16)[:, 0:4 * XP].rearrange("p (k y h) -> p k y h", k=4, h=2)
                    dst = xT[:, 1:1 + IMG, 1:1 + IMG].rearrange("p y (h k) -> p k y h", h=2)[:, 4 * g:4 * g + 4]
                    for k in range(4):
                        i = act.activation(dst[:, k], src[:, k], ACT.Copy)
                    i.then_inc(S["xt_ready"], 1)

            act.wait_ge(S["wscale"], 1)
            for t in range(STEPS):
                prepare(0, t)
            with act.Fori(0, PAIRS) as p:
                for t in range(NW + 3):
                    if t < NW:
                        act.wait_ge(S["conv_full"], p * NW + t + 1)
                        act.activation(x1[:, t], ps[:, 0, 0:ST], ACT.Identity, scale=cscale[:], bias=bconv).then_inc(S["x1_ready"], 1)
                    if 0 <= t - 1 < NW:
                        s = t - 1
                        act.wait_ge(S["xc_ready"], 1 + p * NW + s + 1)
                        act.activation(sq[:, s % 2], xn[:, s], ACT.Square).then_inc(S["sq_ready"], 1)
                    if 0 <= t - 2 < NW:
                        s = t - 2
                        act.wait_ge(S["var_full"], p * NW + s + 1)
                        act.wait_ge(S["rs_ready"], 1 + p * NW + s)
                        if s == 0:
                            act.wait_ge(S["out_stored"], 1 + p * (NW * 32))
                        act.activation(lnv[:], ps[:, 2, 0:ST], ACT.Ln, bias=epst[:]).then_inc(S["lnv_ready"], 1)
                        act.wait_ge(S["lnv_ready"], 1 + p * NW + s + 1)
                        act.activation(rs[:, s % 2], lnv[:], ACT.Exp, scale=-0.5).then_inc(S["rs_ready"], 1)
                    if 0 <= t - 3 < NW:
                        s = t - 3
                        n = p * NW + s + 1
                        act.wait_ge(S["q_full"], n)
                        act.activation(qH[:, s], ps[:, 3, 0:ST], ACT.Identity, bias=bq).then_inc(S["qH_ready"], 1)
                        act.wait_ge(S["k_full"], n)
                        b = s % 2
                        per = len(range(b, NW, 2))
                        if s >= 2:
                            act.wait_ge(ks_stored[b], 1 + p * (128 * per) + 128 * (s // 2))
                            act.wait_ge(kl_stored[b], p * (64 * per) + 64 * (s // 2))
                        act.activation(kH[:, b], ps[:, 4, 0:ST], ACT.Identity, bias=bk).then_inc(S["kH_ready"], 1)

                attend(p, 0, "first")
                with act.Fori(1, NW) as s:
                    attend(p, s, "middle")
                attend(p, NW, "end")

        @block.tensor
        def _(pe):
            for name in 'st_full u_full mt_full'.split():
                pe.sem_inc(S[name], 1)
            def finish(p, s, t):
                U = p * NW + s
                if t == 1:
                    pe.wait_ge(S["u_ready"], 1 + U * NW + NW)
                    pe.wait_ge(S["ot_ready"], 1 + U)
                if 1 <= t < 5:
                    i = t - 1
                    if i >= 2:
                        pe.wait_ge(S["lns_ready"], U * 4 + i - 1)
                    pe.matmul(ps[:, 6 + i % 2, 0:ST], pick[:], us[:, i // 2, i % 2], start=True, stop=True).then_inc(S["sum_full"], 1)
                if t == 6:
                    pe.wait_ge(S["lns_ready"], U * 4 + 3)
                    pe.wait_ge(S["un_ready"], U * 4 + 4)
                    for e in range(2):
                        for h in range(2):
                            i = pe.matmul(ps[64 * h:64 * h + 64, 6, 0:ST], wo[:, e, :], un[:, h, e], start=e == 0, stop=e == 1)
                    i.then_inc(S["y_full"], 1)
                if t == 7:
                    pe.wait_ge(S["lns_ready"], U * 4 + 4)
                    pe.wait_ge(S["x2_ready"], U + 1)
                    pe.matmul(ps[:, 7, 0:ST], center_w[:], x2[:], start=True, stop=True).then_inc(S["xc2_full"], 1)
                if t == 8:
                    pe.wait_ge(S["sq2_ready"], U + 1)
                    pe.matmul(ps[:, 6, 0:ST], mean_w[:], st2[:], start=True, stop=True).then_inc(S["var2_full"], 1)
                if t in (10, 11):
                    pe.wait_ge(S["xn2_ready"], U + 1)
                    h = t - 10
                    for m in range(2):
                        if h == 1:
                            pe.wait_ge(S["z_ready"], U * 2 + m + 1)
                        pe.matmul(ps[:, 6 + m, 0:ST], w1[:, h, 128 * m:128 * m + 128], nm2[:], start=True, stop=True).then_inc(S["h_full"], 1)
                if t == 12:
                    for h in (1, 0):
                        pe.wait_ge(S["hid_ready"], U * 4 + (2 if h else 4))
                        for m in range(2):
                            i = pe.matmul(ps[64 * h:64 * h + 64, 6, 0:ST], w2[:, m, :], hid[:, 2 * h + m], start=m == 0, stop=m == 1)
                    i.then_inc(S["o_full"], 1)
                if t == 13:
                    pe.wait_ge(S["x3_ready"], U + 1)
                    for k in range(4):
                        i = pe.transpose(ps[0:OT, 7, 128 * k:128 * k + 128], x3[:, OT * k:OT * k + OT], ident[:])
                    i.then_inc(S["t_full"], 1)

            def attend(p, s, kind):
                T = p * NW + s
                G = T * STEPS
                for t in range(STEPS):
                    if kind != "end":
                        b = SLOT[t]
                        pe.wait_ge(S["qb_ready"], 1 + G + t + 1)
                        pe.wait_ge(S["qc_ready"], 1 + T * len(POOL_STEPS) + by_pool(t + 1))
                        pe.wait_ge(S["mx_ready"], 1 + G + t)
                        for g in range(NG):
                            for j in range(2):
                                i = pe.matmul(ps[:, g, 256 * j:256 * j + 256],
                                              qb[b][:, g, 2 * j:2 * j + 2, :].rearrange("p h t -> p (h t)"),
                                              kg[b][:, g].rearrange("p k t -> p (k t)"), start=True, stop=True)
                        i.then_inc(S["sm_full"], 1)
                    if here(t - 2, kind):
                        i0 = t - 2
                        h, b = i0 % 2, SLOT[i0]
                        pe.wait_ge(S["vg_ready"], 1 + G + i0 + 1)
                        pe.wait_ge(S["pt_ready"], 1 + (G + i0 + 1) * 2)
                        if h == 0:
                            pe.wait_ge(S["u_ready"], 1 + T * NW + i0 // 2)
                        for c in range(2):
                            for j in range(4):
                                i = pe.matmul(ps[32 * j:32 * j + 32, 5, 128 * h:128 * h + 128],
                                              vg[b][:, c * 4 * VC + VC * j:c * 4 * VC + VC * j + 32],
                                              pt[i0 % 2][:, c, 128 * j:128 * j + 128], start=c == 0, stop=c == 1)
                        i.then_inc(S["u_full"], 1)
                    if kind != "first" and t not in LATE:
                        finish(p, s - 1, t)
                    if here(t - 1, kind):
                        i0 = t - 1
                        b = SLOT[i0]
                        pe.wait_ge(S["mt_ready"], 1 + G + i0 + 1)
                        for c in range(2):
                            pe.wait_ge(S["pt_ready"], 1 + (G + i0) * 2)
                            for g in range(NG):
                                i = pe.matmul(ps[:, 2 + c, 256 * g:256 * g + 256],
                                              kg[b][:, g, 2 * c:2 * c + 2, :].rearrange("p k t -> p (k t)"),
                                              qb[b][:, g].rearrange("p h t -> p (h t)"), start=True, stop=True)
                            i.then_inc(S["st_full"], 1)
                    if kind != "end":
                        pe.wait_ge(S["mx_ready"], 1 + G + t + 1)
                        pe.wait_ge(S["mt_ready"], 1 + G + t)
                        for j in range(4):
                            i = pe.matmul(ps[NP3:NP3 + 1, 4, 128 * j:128 * j + 128], mx[t % 2][:, j:j + 1], identb[:], start=True, stop=True)
                        i.then_inc(S["mt_full"], 1)
                    if kind != "first":
                        if t in LATE:
                            finish(p, s - 1, t)
                    if kind == "end":
                        prepare(p + 1, t)

            def prepare(n, t):
                for g in {9: (0, 1), 10: (2,), 11: (3,), 12: (4, 5), 13: (6,)}.get(t, ()):
                    if g == 0:
                        pe.wait_ge(S["x_ready"], 1 + n * 2 + 2)
                    if g >= 2:
                        pe.wait_ge(S["xt_ready"], n * 7 + g - 1)
                    for k in range(4):
                        i = pe.transpose(ps[:, g % 2, :].bitcast(BF16)[:, k * XP:(k + 1) * XP], xq[:, 4 * g + k, :], identb[0:XP, 0:XP])
                    i.then_inc(S["xt_full"], 1)

            pe.wait_ge(S["wabs"], 1)
            pe.matmul(ps[:, 0, 0:1], mean_w[:], wsum[:], start=True, stop=True).then_inc(S["wsum_full"], 1)
            pe.wait_ge(S["wscale"], 1)
            pe.wait_ge(S["sign_ready"], 1)
            for t in range(STEPS):
                prepare(0, t)
            with pe.Fori(0, PAIRS) as p:
                pe.wait_ge(S["xt_ready"], p * 7 + 7)
                for t in range(NW + 3):
                    if t < NW:
                        pe.wait_ge(S["x1_ready"], 1 + p * NW + t)
                        for tap in range(9):
                            dy, dx = tap // 3, tap % 3
                            rhs = xT[:, t * WS + dy:t * WS + dy + WS, dx:dx + IMG].rearrange("p y (n c) -> p n y c", n=NW)
                            i = pe.matmul(ps[:, 0, 0:ST].rearrange("p (n y c) -> p n y c", n=NW, y=WS), wconv[:, tap, :], rhs, start=tap == 0, stop=tap == 8)
                        i.then_inc(S["conv_full"], 1)
                    if 0 <= t - 1 < NW:
                        s = t - 1
                        pe.wait_ge(S["x1_ready"], 1 + p * NW + s + 1)
                        pe.wait_ge(S["xc_ready"], 1 + p * NW + s)
                        pe.matmul(ps[:, 1, 0:ST], mean_w[:], x1[:, s], start=True, stop=True).then_inc(S["mean_full"], 1)
                    if 0 <= t - 2 < NW:
                        s = t - 2
                        pe.wait_ge(S["sq_ready"], p * NW + s + 1)
                        pe.wait_ge(S["lnv_ready"], 1 + p * NW + s)
                        pe.matmul(ps[:, 2, 0:ST], mean_w[:], sq[:, s % 2], start=True, stop=True).then_inc(S["var_full"], 1)
                    if 0 <= t - 3 < NW:
                        s = t - 3
                        n = p * NW + s
                        pe.wait_ge(S["xn_ready"], n + 1)
                        pe.wait_ge(S["qL_ready"], 1 + n)
                        pe.matmul(ps[:, 3, 0:ST], wq[:], xn[:, s], start=True, stop=True).then_inc(S["q_full"], 1)
                        pe.wait_ge(S["kL_ready"], 1 + n)
                        pe.matmul(ps[:, 4, 0:ST], wk[:], xn[:, s], start=True, stop=True).then_inc(S["k_full"], 1)
                        pe.wait_ge(S["v_ready"], 1 + n)
                        for w in range(NW):
                            for d in (0, 64):
                                i = pe.matmul(ps[d:d + 64, 5 + w // 4, 128 * (w % 4):128 * (w % 4) + 128],
                                              xn[:, s, w * RT:w * RT + RT], wv[:], start=True, stop=True)
                        i.then_inc(S["v_full"], 1)
                pe.wait_ge(S["logit_ready"], p * 2 + 1)
                settled(pe)
                for h in range(2):
                    d = slice(64 * h, 64 * h + 64)
                    i = pe.matmul(ps[0:R, h, 0:R], regsum[d, 0, :], regsum[d, 1, :], start=True, stop=True)
                i.then_inc(S["logit_full"], 1)
                pe.wait_ge(S["v_ready"], 1 + p * NW + NW)
                pe.wait_ge(S["logit_ready"], p * 2 + 2)
                settled(pe)

                attend(p, 0, "first")
                with pe.Fori(1, NW) as s:
                    attend(p, s, "middle")
                attend(p, NW, "end")


WEIGHT_DMAS = 12 + 16 + 1 + 4 + 8

_INS = ["x", "L0_conv_W", "L0_conv_b", "L1_conv_ln1_g", "L1_conv_ln1_b", "L1_conv_wqkv", "L1_conv_bqkv",
        "L1_conv_wo", "L1_conv_bo", "L1_conv_ln2_g", "L1_conv_ln2_b", "L1_conv_w1", "L1_conv_bm1",
        "L1_conv_w2", "L1_conv_bm2"]


def kernel(**inputs):
    import numpy as _np
    import concourse.bacc as _bacc
    from concourse import mybir as _mybir
    from concourse.bass_utils import run_bass_kernel_spmd as _run

    nc = _bacc.Bacc("TRN2", target_bir_lowering=False, num_devices=1)
    arrays, io = {}, {}
    for name in _INS:
        a = _np.ascontiguousarray(inputs[name])
        arrays[f"in_{name}"] = a
        io[name] = nc.dram_tensor(f"in_{name}", a.shape, _mybir.dt.from_np(a.dtype), kind="ExternalInput").ap()
    io["out"] = nc.dram_tensor("out_0", inputs["x"].shape, _mybir.dt.float32, kind="ExternalOutput").ap()
    build(nc, io)
    r = _run(nc, [arrays], core_ids=[0])
    return r.results[0]["out_0"]
```
